# Optimizing a Trainium2 kernel written in Bass

```python
import numpy as np
import jax
import jax.numpy as jnp

def _softmax(x, axis=-1):
    return jax.nn.softmax(x, axis=axis)

def _gelu(x):
    return jax.nn.gelu(x, approximate=True)

def _silu(x):
    return jax.nn.silu(x)

def _sigmoid(x):
    return jax.nn.sigmoid(x)

def _layernorm(x, axis=-1, eps=1e-05):
    m = jnp.mean(x, axis=axis, keepdims=True)
    v = jnp.var(x, axis=axis, keepdims=True)
    return (x - m) / jnp.sqrt(v + eps)

def _scatter_add(tgt, idx, src, axis=0):
    return tgt.at[idx].add(src)

def _segment_sum(src, seg, n):
    return jax.ops.segment_sum(src, seg, n)
kernel_name = 'mk_dlrm_tower_d1_rec_r8_ae7144'

def setup_inputs(seed: int=0):
    np.random.seed(seed)
    _w = jnp.asarray

    def _rec_inputs():
        import jax
        import jax.numpy as jnp
        _tk = jax.random.key(seed)
        ids = jnp.stack([jax.random.randint(jax.random.fold_in(_tk, 200 + f), (2048,), 0, v, jnp.int32) for f, v in enumerate([1250, 1250, 1000, 125000, 12500, 1000, 1250, 1250, 12500, 1250, 1000, 1250, 1000, 1000, 1000, 1000, 1250, 1250, 12500, 1000, 1250, 12500, 1250, 1000, 12500, 1000])], axis=1)
        tbl_0 = 0.05 * jax.random.normal(jax.random.fold_in(_tk, 500 + 0), (1250, 128), jnp.float32)
        tbl_1 = 0.05 * jax.random.normal(jax.random.fold_in(_tk, 500 + 1), (1250, 128), jnp.float32)
        tbl_2 = 0.05 * jax.random.normal(jax.random.fold_in(_tk, 500 + 2), (1000, 128), jnp.float32)
        tbl_3 = 0.05 * jax.random.normal(jax.random.fold_in(_tk, 500 + 3), (125000, 128), jnp.float32)
        tbl_4 = 0.05 * jax.random.normal(jax.random.fold_in(_tk, 500 + 4), (12500, 128), jnp.float32)
        tbl_5 = 0.05 * jax.random.normal(jax.random.fold_in(_tk, 500 + 5), (1000, 128), jnp.float32)
        tbl_6 = 0.05 * jax.random.normal(jax.random.fold_in(_tk, 500 + 6), (1250, 128), jnp.float32)
        tbl_7 = 0.05 * jax.random.normal(jax.random.fold_in(_tk, 500 + 7), (1250, 128), jnp.float32)
        tbl_8 = 0.05 * jax.random.normal(jax.random.fold_in(_tk, 500 + 8), (12500, 128), jnp.float32)
        tbl_9 = 0.05 * jax.random.normal(jax.random.fold_in(_tk, 500 + 9), (1250, 128), jnp.float32)
        tbl_10 = 0.05 * jax.random.normal(jax.random.fold_in(_tk, 500 + 10), (1000, 128), jnp.float32)
        tbl_11 = 0.05 * jax.random.normal(jax.random.fold_in(_tk, 500 + 11), (1250, 128), jnp.float32)
        tbl_12 = 0.05 * jax.random.normal(jax.random.fold_in(_tk, 500 + 12), (1000, 128), jnp.float32)
        tbl_13 = 0.05 * jax.random.normal(jax.random.fold_in(_tk, 500 + 13), (1000, 128), jnp.float32)
        tbl_14 = 0.05 * jax.random.normal(jax.random.fold_in(_tk, 500 + 14), (1000, 128), jnp.float32)
        tbl_15 = 0.05 * jax.random.normal(jax.random.fold_in(_tk, 500 + 15), (1000, 128), jnp.float32)
        tbl_16 = 0.05 * jax.random.normal(jax.random.fold_in(_tk, 500 + 16), (1250, 128), jnp.float32)
        tbl_17 = 0.05 * jax.random.normal(jax.random.fold_in(_tk, 500 + 17), (1250, 128), jnp.float32)
        tbl_18 = 0.05 * jax.random.normal(jax.random.fold_in(_tk, 500 + 18), (12500, 128), jnp.float32)
        tbl_19 = 0.05 * jax.random.normal(jax.random.fold_in(_tk, 500 + 19), (1000, 128), jnp.float32)
        tbl_20 = 0.05 * jax.random.normal(jax.random.fold_in(_tk, 500 + 20), (1250, 128), jnp.float32)
        tbl_21 = 0.05 * jax.random.normal(jax.random.fold_in(_tk, 500 + 21), (12500, 128), jnp.float32)
        tbl_22 = 0.05 * jax.random.normal(jax.random.fold_in(_tk, 500 + 22), (1250, 128), jnp.float32)
        tbl_23 = 0.05 * jax.random.normal(jax.random.fold_in(_tk, 500 + 23), (1000, 128), jnp.float32)
        tbl_24 = 0.05 * jax.random.normal(jax.random.fold_in(_tk, 500 + 24), (12500, 128), jnp.float32)
        tbl_25 = 0.05 * jax.random.normal(jax.random.fold_in(_tk, 500 + 25), (1000, 128), jnp.float32)
        _rk = jax.random.fold_in(_tk, 7)
        r_dense_features = -0.000292821 + 1.00034 * jax.random.normal(jax.random.fold_in(_rk, 101), (2048, 128), jnp.float32)
        W_top1 = 0.0405887 * jax.random.normal(jax.random.fold_in(_tk, 801), (607, 512), jnp.float32)
        W_top2 = 0.0441942 * jax.random.normal(jax.random.fold_in(_tk, 802), (512, 256), jnp.float32)
        W_top3 = 0.0625 * jax.random.normal(jax.random.fold_in(_tk, 803), (256, 1), jnp.float32)
        b_top1 = jnp.zeros((512,), jnp.float32)
        b_top2 = jnp.zeros((256,), jnp.float32)
        return (r_dense_features, ids, tbl_0, tbl_1, tbl_2, tbl_3, tbl_4, tbl_5, tbl_6, tbl_7, tbl_8, tbl_9, tbl_10, tbl_11, tbl_12, tbl_13, tbl_14, tbl_15, tbl_16, tbl_17, tbl_18, tbl_19, tbl_20, tbl_21, tbl_22, tbl_23, tbl_24, tbl_25, W_top1, b_top1, W_top2, b_top2, W_top3)
    r_dense_features, ids, tbl_0, tbl_1, tbl_2, tbl_3, tbl_4, tbl_5, tbl_6, tbl_7, tbl_8, tbl_9, tbl_10, tbl_11, tbl_12, tbl_13, tbl_14, tbl_15, tbl_16, tbl_17, tbl_18, tbl_19, tbl_20, tbl_21, tbl_22, tbl_23, tbl_24, tbl_25, W_top1, b_top1, W_top2, b_top2, W_top3 = _rec_inputs()

    def _L0_rec_setup():
        import jax, jax.numpy as jnp
        import numpy as np
        F = 26
        _TRIU_I, _TRIU_J = np.triu_indices(F + 1, k=1)
        key = jax.random.key(seed)
        k1, k2 = jax.random.split(key)
        B, D = (4096, 128)
        dense_features = jax.random.normal(k1, (B, D), dtype=jnp.float32)
        sparse_features = jax.random.normal(k2, (B, F, D), dtype=jnp.float32)
        return {'dense_features': dense_features, 'sparse_features': sparse_features}
    _L0_rec_all = _L0_rec_setup()
    _L0_rec_in = {k: v for k, v in _L0_rec_all.items() if k in ()}
    del _L0_rec_all
    return {'r_dense_features': r_dense_features, 'ids': ids, 'tbl_0': tbl_0, 'tbl_1': tbl_1, 'tbl_2': tbl_2, 'tbl_3': tbl_3, 'tbl_4': tbl_4, 'tbl_5': tbl_5, 'tbl_6': tbl_6, 'tbl_7': tbl_7, 'tbl_8': tbl_8, 'tbl_9': tbl_9, 'tbl_10': tbl_10, 'tbl_11': tbl_11, 'tbl_12': tbl_12, 'tbl_13': tbl_13, 'tbl_14': tbl_14, 'tbl_15': tbl_15, 'tbl_16': tbl_16, 'tbl_17': tbl_17, 'tbl_18': tbl_18, 'tbl_19': tbl_19, 'tbl_20': tbl_20, 'tbl_21': tbl_21, 'tbl_22': tbl_22, 'tbl_23': tbl_23, 'tbl_24': tbl_24, 'tbl_25': tbl_25, 'W_top1': W_top1, 'b_top1': b_top1, 'W_top2': W_top2, 'b_top2': b_top2, 'W_top3': W_top3}

def reference(r_dense_features, ids, tbl_0, tbl_1, tbl_2, tbl_3, tbl_4, tbl_5, tbl_6, tbl_7, tbl_8, tbl_9, tbl_10, tbl_11, tbl_12, tbl_13, tbl_14, tbl_15, tbl_16, tbl_17, tbl_18, tbl_19, tbl_20, tbl_21, tbl_22, tbl_23, tbl_24, tbl_25, W_top1, b_top1, W_top2, b_top2, W_top3):
    import jax
    import jax.numpy as jnp

    def _L0_rec_ref(dense_features, sparse_features):
        import jax, jax.numpy as jnp
        import numpy as np
        F = 26
        _TRIU_I, _TRIU_J = np.triu_indices(F + 1, k=1)
        combined = jnp.concatenate([dense_features[:, None, :], sparse_features], axis=1)
        interactions = jnp.einsum('bfd,bgd->bfg', combined, combined)
        interactions_flat = interactions[:, _TRIU_I, _TRIU_J]
        return jnp.concatenate([dense_features, interactions_flat], axis=1)
    e = jnp.stack([tbl_0[ids[:, 0]], tbl_1[ids[:, 1]], tbl_2[ids[:, 2]], tbl_3[ids[:, 3]], tbl_4[ids[:, 4]], tbl_5[ids[:, 5]], tbl_6[ids[:, 6]], tbl_7[ids[:, 7]], tbl_8[ids[:, 8]], tbl_9[ids[:, 9]], tbl_10[ids[:, 10]], tbl_11[ids[:, 11]], tbl_12[ids[:, 12]], tbl_13[ids[:, 13]], tbl_14[ids[:, 14]], tbl_15[ids[:, 15]], tbl_16[ids[:, 16]], tbl_17[ids[:, 17]], tbl_18[ids[:, 18]], tbl_19[ids[:, 19]], tbl_20[ids[:, 20]], tbl_21[ids[:, 21]], tbl_22[ids[:, 22]], tbl_23[ids[:, 23]], tbl_24[ids[:, 24]], tbl_25[ids[:, 25]]], axis=1)
    z = _L0_rec_ref(r_dense_features, e)
    z = z.reshape(z.shape[0], -1)
    h = jnp.concatenate([z, r_dense_features], axis=1)
    h = jnp.maximum(h @ W_top1 + b_top1, 0.0)
    h = jnp.maximum(h @ W_top2 + b_top2, 0.0)
    y = h @ W_top3
    return y

_drawn_inputs = setup_inputs


def setup_inputs(seed=0):
    import zlib

    import numpy as np

    out = dict(_drawn_inputs(seed))
    spreads = {'b_top1': (0.0, 0.1), 'b_top2': (0.0, 0.1)}
    factors = {}
    for name, (base, spread) in spreads.items():
        noise = np.random.default_rng([zlib.crc32(name.encode()), seed]).standard_normal(out[name].shape)
        drawn = base * np.exp(spread * noise) if base else spread * noise
        out[name] = jnp.asarray(drawn.astype(out[name].dtype))
    for name, factor in factors.items():
        out[name] = (out[name] * factor).astype(out[name].dtype)
    return out
```

```python
from contextlib import ExitStack

import concourse.bass as bass
from concourse import mybir

F32 = mybir.dt.float32
F32R = mybir.dt.float32r
I32 = mybir.dt.int32
U32 = mybir.dt.uint32
ALU = mybir.AluOpType
ACT = mybir.ActivationFunctionType

P = 128
LOOKUP_TABLES = [2, 5, 10, 12, 13, 14, 15]


def build(nc, aps, out):
    ids = aps["ids"]
    B, NTAB = ids.shape
    D = aps["r_dense_features"].shape[1]
    assert D == P
    F = NTAB + 1
    H1 = aps["W_top1"].shape[1]
    H2 = aps["W_top2"].shape[1]
    PAIRS = F * (F - 1) // 2

    TILE = P
    HALF = 2 * TILE
    CHUNK = 2 * HALF
    NCHUNK = B // CHUNK
    NTILE = B // TILE
    NL = len(LOOKUP_TABLES)
    GATHER_TABLES = [f for f in range(NTAB) if f not in LOOKUP_TABLES]
    NG = len(GATHER_TABLES)
    ROWS_PER_PART = aps[f"tbl_{LOOKUP_TABLES[0]}"].shape[0] // 125
    VP = 125
    KT = ROWS_PER_PART
    assert all(aps[f"tbl_{f}"].shape[0] == VP * KT for f in LOOKUP_TABLES)

    QUAD = 4
    QW = 32
    NA = F - 1
    GROUPS_STEP = 8
    STEPS = HALF // QUAD // GROUPS_STEP
    PER_BANK = 4
    K_PAIR = [(k, min(P, PAIRS - k)) for k in range(0, PAIRS, P)]
    T_BANKS = 8
    A_OF = [range(NA * b // T_BANKS, NA * (b + 1) // T_BANKS) for b in range(T_BANKS)]
    PAIR0 = [F * a - a * (a + 1) // 2 for a in range(F)]

    FEAT = [0] + [f + 1 for f in GATHER_TABLES]
    XGROUPS = [list(range(g, min(g + 4, len(FEAT)))) for g in range(1, len(FEAT), 4)]
    USES_X = 1 + len(XGROUPS)
    USES_MLP = T_BANKS + len(K_PAIR) + H1 // P + H2 // P + 1
    USES_HALF = 2 * USES_X + NL
    USES = 2 * USES_HALF + USES_MLP
    BASE = NTILE // 4 + NL
    assert USES % 2 == 0 and NL <= STEPS and B % CHUNK == 0

    def x_done(c, t):
        h, q = divmod(t, 2)
        between = 0 if q == 0 or (h == 1 and isinstance(c, int) and c == NCHUNK - 1) else min(NL, STEPS // 2)
        return c * USES + BASE + h * USES_HALF + USES_X * (q + 1) + between

    def lookup_done(c, h, m):
        return c * USES + BASE + h * USES_HALF + USES_X * (1 if m < STEPS // 2 else 2) + m + 1

    def runs(slots):
        i = 0
        while i < len(slots):
            n = 1
            while i + n < len(slots) and slots[i + n] - slots[i + n - 1] == slots[min(i + 1, len(slots) - 1)] - slots[i]:
                n += 1
            yield i, slots[i], (slots[i + 1] - slots[i] if n > 1 else 1), n
            i += n

    with ExitStack() as ctx:
        def sb(name, shape, dt=F32):
            return ctx.enter_context(nc.sbuf_tensor(name, shape, dt))

        def sem(name):
            return ctx.enter_context(nc.semaphore(name))

        ident = sb("ident", [P, P])
        ident_r = sb("ident_r", [P, P], F32R)
        ids_t = sb("ids_t", [NTAB, B], F32R)
        ids_tile = sb("ids_tile", [P, 4, NTAB], I32)
        vrow_i = sb("vrow_i", [VP, KT], I32)
        vrow = sb("vrow", [VP, KT])
        table_hi = sb("table_hi", [VP, NL, KT, D], F32R)
        table_lo = sb("table_lo", [VP, NL, KT, D], F32R)
        onehot = sb("onehot", [VP, 2, KT, HALF], F32R)
        rows = sb("rows", [P, 2, 1 + NG, D])
        XT = [sb(f"xt{h}", [D, HALF, QW]) for h in range(2)]
        A = sb("A", [P, NA, P])
        pairs_or_h1 = sb("pairs_or_h1", [P, max(QUAD * PAIRS, H1 // P * CHUNK)])
        pairs_t_or_h2 = sb("pairs_t_or_h2", [P, max(len(K_PAIR), H2 // P) * CHUNK])
        dense_t = sb("dense_t", [D, CHUNK])
        w1_dense = sb("w1_dense", [D, H1])
        w1_pair = sb("w1_pair", [P, len(K_PAIR), H1])
        w2 = sb("w2", [P, H1 // P, H2])
        w3 = sb("w3", [P, H2 // P])
        b1 = sb("b1", [P, H1 // P])
        b2 = sb("b2", [P, H2 // P])

        pairs = pairs_or_h1[:, 0:QUAD * PAIRS].rearrange("p (j x) -> p j x", j=QUAD)
        h1 = pairs_or_h1[:, 0:H1 // P * CHUNK].rearrange("p (n s) -> p n s", s=CHUNK)
        pairs_t = pairs_t_or_h2[:, 0:len(K_PAIR) * CHUNK].rearrange("p (k s) -> p k s", s=CHUNK)
        h2 = pairs_t_or_h2[:, 0:H2 // P * CHUNK].rearrange("p (n s) -> p n s", s=CHUNK)
        y_row = pairs_t_or_h2[0:1, H2 // P * CHUNK:(H2 // P + 1) * CHUNK]
        raw = A[:].rearrange("p a s -> p (a s)")[0:VP, 0:2 * KT * D].rearrange("p (u k d) -> p u k d", u=2, k=KT)
        spare = A[:].rearrange("p a s -> p (a s)")[:, 2 * KT * D:]
        ids_all = dense_t[:, 0:NTILE * NTAB].bitcast(I32).rearrange("p (t f) -> p t f", f=NTAB)
        w1_again = spare[:, 0:H1]
        ids_f = spare[:, H1:H1 + NTILE * NTAB].rearrange("p (t f) -> p t f", f=NTAB)

        ring = ctx.enter_context(nc.psum_tensor("ring", [P, 2, 512], F32))
        idb = ctx.enter_context(nc.psum_tensor("idb", [P, 2, 512], F32))
        gram = ctx.enter_context(nc.psum_tensor("gram", [P, 2, 2, 512], F32))

        ids_landed = sem("ids_landed")
        ids_slot = [sem(f"ids_slot{t}") for t in range(4)]
        rows_landed = [sem(f"rows_landed{q}") for q in range(2)]
        dense_landed = [sem(f"dense_landed{q}") for q in range(2)]
        weights_landed = sem("weights_landed")
        raw_landed = [sem(f"raw_landed{u}") for u in range(2)]
        const_ready = sem("const_ready")
        cleared = sem("cleared")
        ids_f_ready = sem("ids_f_ready")
        ident_r_ready = sem("ident_r_ready")
        vrow_ready = sem("vrow_ready")
        hi_ready = sem("hi_ready")
        lo_ready = sem("lo_ready")
        w1_ready = sem("w1_ready")
        filled = sem("filled")
        emptied = sem("emptied")
        idb_ready = sem("idb_ready")
        onehot_ready = sem("onehot_ready")
        gram_ready = sem("gram_ready")
        gram_act = sem("gram_act")
        gram_dve = sem("gram_dve")
        y_stored = sem("y_stored")
        tiles_begun = sem("tiles_begun")
        block = ctx.enter_context(nc.Block())

        def product_views(h, s, j):
            g0 = (h * STEPS + s) * GROUPS_STEP
            dst = A[QW * j:QW * j + F, :, g0:g0 + GROUPS_STEP].rearrange("b a (u g) -> b u g a", g=PER_BANK)
            src = gram[QW * j:QW * j + F, s % 2, :, 0:PER_BANK * QUAD * NA].rearrange(
                "b u (g x) -> b u g x", g=PER_BANK)[:, :, :, NA * j:NA * (j + 1)]
            return dst, src

        @block.sync
        def _(sp):
            def load_ids(c, t):
                src = ids[bass.ds(c * CHUNK + t * TILE, TILE), :]
                sp.dma_start(ids_tile[:, t, :], src).then_inc(ids_slot[t], 16)

            def load_dense(c, t):
                src = aps["r_dense_features"][bass.ds(c * CHUNK + t * TILE, TILE), :]
                sp.dma_start(rows[:, t % 2, 0, :], src).then_inc(dense_landed[t % 2], 16)

            def tiles(c, ts, more_ids=True):
                for dc, t in ts:
                    sp.wait_ge(filled, x_done(c + dc - (1 if t < 2 else 0), (t + 2) % 4))
                    load_dense(c + dc, t)

            for t in range(4):
                load_ids(0, t)
            sp.dma_start(ids_all[:], ids.rearrange("(t p) f -> p t f", p=P)).then_inc(ids_landed, 16)
            load_dense(0, 0)
            load_dense(0, 1)
            sp.wait_ge(cleared, 1)
            for j, f in enumerate(LOOKUP_TABLES):
                if j >= 2:
                    sp.wait_ge(hi_ready, j - 1)
                    sp.wait_ge(lo_ready, j - 1)
                sp.dma_start(raw[:, j % 2], aps[f"tbl_{f}"].rearrange("(p k) d -> p k d", k=KT)).then_inc(raw_landed[j % 2], 16)
            W1, W2 = aps["W_top1"], aps["W_top2"]
            sp.dma_start(w1_dense[:], W1[0:D, :]).then_inc(weights_landed, 16)
            sp.dma_start(w1_again[:], W1[D + PAIRS:2 * D + PAIRS, :]).then_inc(weights_landed, 16)
            for k, (k0, w) in enumerate(K_PAIR):
                sp.dma_start(w1_pair[0:w, k, :], W1[D + k0:D + k0 + w, :]).then_inc(weights_landed, 16)
            sp.dma_start(w2[:], W2.rearrange("(k p) n -> p k n", p=P)).then_inc(weights_landed, 16)
            with nc.allow_non_contiguous_dma(reason="biases and W3: a few hundred single values, once"):
                sp.dma_start(w3[:], aps["W_top3"].rearrange("(k p) o -> p (k o)", p=P)).then_inc(weights_landed, 16)
                sp.dma_start(b1[:], aps["b_top1"].rearrange("(n p) -> p n", p=P)).then_inc(weights_landed, 16)
                sp.dma_start(b2[:], aps["b_top2"].rearrange("(n p) -> p n", p=P)).then_inc(weights_landed, 16)

            def next_ids(c, t):
                sp.wait_ge(rows_landed[t % 2], 16 * NG * (2 * c + t // 2 + 1))
                load_ids(c + 1, t)

            with sp.Fori(0, NCHUNK - 1) as c:
                tiles(c, [(0, 2)])
                next_ids(c, 0)
                tiles(c, [(0, 3)])
                next_ids(c, 1)
                tiles(c, [(1, 0)])
                next_ids(c, 2)
                tiles(c, [(1, 1)])
                next_ids(c, 3)
            tiles(NCHUNK - 1, [(0, 2), (0, 3)])

        @block.gpsimd
        def _(pool):
            def gathers(c, t):
                pool.wait_ge(ids_slot[t], 16 * (c + 1))
                pool.sem_inc(tiles_begun, 1)
                for r, f in enumerate(GATHER_TABLES):
                    pool.indirect_dma_start(
                        rows[:, t % 2, 1 + r, :], None, aps[f"tbl_{f}"],
                        bass.IndirectOffsetOnAxis(ap=ids_tile[:, t, f:f + 1].bitcast(U32), axis=0),
                    ).then_inc(rows_landed[t % 2], 16)

            def gathers_after(c, dc, t):
                pool.wait_ge(filled, x_done(c + dc - (1 if t < 2 else 0), (t + 2) % 4))
                gathers(c + dc, t)

            pool.iota(vrow_i[:], pattern=[[1, KT]], base=0, channel_multiplier=KT).then_inc(const_ready, 1)
            pool.memset(ident[:], 0.0).then_inc(const_ready, 1)
            pool.wait_ge(const_ready, 2)
            pool.affine_select(out=ident[:], in_=ident[:], compare_op=ALU.not_equal, fill=1.0, base=0,
                               pattern=[[-1, P]], channel_multiplier=1).then_inc(const_ready, 1)
            gathers(0, 0)
            gathers(0, 1)
            with pool.Fori(0, NCHUNK - 1) as c:
                gathers_after(c, 0, 2)
                gathers_after(c, 0, 3)
                gathers_after(c, 1, 0)
                gathers_after(c, 1, 1)
            gathers_after(NCHUNK - 1, 0, 2)
            gathers_after(NCHUNK - 1, 0, 3)

        @block.tensor
        def _(pe):
            use = [0]

            def claim(c, base):
                n = use[0]
                use[0] += 1
                if not isinstance(c, int) or c * USES + base + n >= 2:
                    pe.wait_ge(emptied, c * USES + base + n - 1)
                return ring[:, (base + n) % 2, :]

            def spread_ids(M, col):
                i = M % NL
                f = LOOKUP_TABLES[i]
                return pe.matmul(idb[:, M % 2, 0:HALF], ident_r[0:NTAB, f:f + 1].to_broadcast([NTAB, P]),
                                 ids_t[:, col], start=True, stop=True)

            def lookup(c, base, m, bank, ready):
                ps = claim(c, base)
                pe.wait_ge(onehot_ready, ready)
                for k in range(KT):
                    for part in (table_hi, table_lo):
                        last = pe.matmul(ps[:, 0:HALF], part[:, m, k, :], onehot[:, bank, k, :],
                                         start=(k == 0 and part is table_hi), stop=(k == KT - 1 and part is table_lo))
                last.then_inc(filled, 1)

            def transpose_rows(c, t):
                q = t % 2
                pe.wait_ge(dense_landed[q], 16 * (2 * c + t // 2 + 1))
                pe.wait_ge(rows_landed[q], 16 * NG * (2 * c + t // 2 + 1))
                for group in [[0]] + XGROUPS:
                    ps = claim(c, BASE)
                    for i, r in enumerate(group):
                        last = pe.transpose(ps[:, i * P:(i + 1) * P], rows[:, q, r, :], ident[:])
                    last.then_inc(filled, 1)

            def products(c, h, s):
                n = 2 * STEPS * c + STEPS * h + s
                if s % (STEPS // 2) == 0:
                    pe.wait_ge(emptied, x_done(c, 2 * h + s // (STEPS // 2)))
                if h == 1 or s >= 2:
                    pe.wait_ge(gram_act, n - 1)
                    pe.wait_ge(gram_dve, n - 1)
                for g in range(GROUPS_STEP):
                    s0 = (s * GROUPS_STEP + g) * QUAD
                    four = XT[h][:, s0:s0 + QUAD, :].rearrange("d j f -> d (j f)")
                    cols = XT[h][:, s0:s0 + QUAD, 0:NA]
                    col = (g % PER_BANK) * QUAD * NA
                    last = pe.matmul(gram[:, s % 2, g // PER_BANK, col:col + QUAD * NA], four, cols,
                                     start=True, stop=True)
                last.then_inc(gram_ready, 1)

            def half(c, h, lookups, last_half=False):
                for s in range(STEPS):
                    if s % (STEPS // 2) == 0:
                        transpose_rows(c, 2 * h + s // (STEPS // 2))
                    products(c, h, s)
                    if lookups and s < NL:
                        M = (h + 1) * NL + s
                        nxt = M + 1
                        if not (last_half and s == NL - 1):
                            col = (c * CHUNK + HALF * (nxt // NL))
                            spread_ids(nxt, bass.ds(col, HALF)).then_inc(idb_ready, 1)
                        lookup(c, BASE, s, M % 2, 2 * NL * c + M + 1)

            def mlp(c):
                pe.wait_ge(gram_act, 2 * STEPS * (c + 1))
                pe.wait_ge(gram_dve, 2 * STEPS * (c + 1))
                for span in A_OF:
                    ps = claim(c, BASE)
                    for i, a in enumerate(span):
                        last = pe.transpose(ps[:, i * P:(i + 1) * P], A[:, a, :], ident[:])
                    last.then_inc(filled, 1)
                pe.wait_ge(emptied, c * USES + BASE + use[0])
                for k, (k0, w) in enumerate(K_PAIR):
                    ps = claim(c, BASE)
                    for j in range(QUAD):
                        last = pe.transpose(ps[0:w, j * P:(j + 1) * P], pairs[:, j, k0:k0 + w], ident[:])
                    last.then_inc(filled, 1)
                pe.wait_ge(w1_ready, 1)
                pe.wait_ge(weights_landed, 16 * N_WEIGHTS)
                pe.wait_ge(emptied, c * USES + BASE + use[0])
                for n in range(H1 // P):
                    ps = claim(c, BASE)
                    cols = slice(n * P, (n + 1) * P)
                    pe.matmul(ps[:], w1_dense[:, cols], dense_t[:], start=True, stop=False)
                    for k, (k0, w) in enumerate(K_PAIR):
                        last = pe.matmul(ps[:], w1_pair[0:w, k, cols], pairs_t[0:w, k, :], start=False,
                                         stop=(k == len(K_PAIR) - 1))
                    last.then_inc(filled, 1)
                pe.wait_ge(emptied, c * USES + BASE + use[0])
                for n in range(H2 // P):
                    ps = claim(c, BASE)
                    for k in range(H1 // P):
                        last = pe.matmul(ps[:], w2[:, k, n * P:(n + 1) * P], h1[:, k, :], start=(k == 0),
                                         stop=(k == H1 // P - 1))
                    last.then_inc(filled, 1)
                pe.wait_ge(emptied, c * USES + BASE + use[0])
                ps = claim(c, BASE)
                for k in range(H2 // P):
                    last = pe.matmul(ps[0:1, :], w3[:, k:k + 1], h2[:, k, :], start=(k == 0), stop=(k == H2 // P - 1))
                last.then_inc(filled, 1)

            pe.wait_ge(const_ready, 3)
            pe.wait_ge(ids_f_ready, 1)
            for t in range(0, NTILE, 4):
                ps = claim(0, 0)
                for i in range(4):
                    last = pe.transpose(ps[0:NTAB, i * P:(i + 1) * P], ids_f[:, t + i, :], ident[:])
                last.then_inc(filled, 1)
            pe.wait_ge(emptied, NTILE // 4)
            pe.wait_ge(ident_r_ready, 1)
            spread_ids(0, slice(0, HALF)).then_inc(idb_ready, 1)
            for m in range(NL):
                nxt = m + 1
                spread_ids(nxt, slice(HALF * (nxt // NL), HALF * (nxt // NL) + HALF)).then_inc(idb_ready, 1)
                pe.wait_ge(hi_ready, m + 1)
                pe.wait_ge(lo_ready, m + 1)
                lookup(0, 0, m, m % 2, m + 1)
            pe.wait_ge(cleared, 3)
            with pe.Fori(0, NCHUNK - 1) as c:
                use[0] = 0
                half(c, 0, True)
                half(c, 1, True)
                mlp(c)
            use[0] = 0
            half(NCHUNK - 1, 0, True, last_half=True)
            half(NCHUNK - 1, 1, False)
            mlp(NCHUNK - 1)

        @block.scalar
        def _(act):
            use = [0]

            def take(c, base):
                n = use[0]
                use[0] += 1
                act.wait_ge(filled, c * USES + base + n + 1)
                return ring[:, (base + n) % 2, :]

            def store_lookup(c, base, h, m):
                ps = take(c, base)
                act.copy(XT[h][:, :, LOOKUP_TABLES[m] + 1], ps[:, 0:HALF]).then_inc(emptied, 1)

            def store_rows(c, t):
                h, q = divmod(t, 2)
                xt = XT[h][:, q * TILE:(q + 1) * TILE, :]
                ps = take(c, BASE)
                act.copy(xt[:, :, 0], ps[:, 0:P])
                g = TILE // QUAD
                act.copy(dense_t[:].rearrange("d (j i) -> d j i", j=QUAD)[:, :, t * g:(t + 1) * g],
                         ps[:, 0:P].rearrange("d (i j) -> d j i", j=QUAD)).then_inc(emptied, 1)
                for group in XGROUPS:
                    ps = take(c, BASE)
                    for i, f0, step, n in runs([FEAT[r] for r in group]):
                        last = act.copy(xt[:, :, f0:f0 + step * (n - 1) + 1:step].rearrange("d s f -> d f s"),
                                        ps[:, i * P:(i + n) * P].rearrange("d (f s) -> d f s", f=n))
                    last.then_inc(emptied, 1)

            def half(c, h, lookups):
                for s in range(STEPS):
                    if s % (STEPS // 2) == 0:
                        store_rows(c, 2 * h + s // (STEPS // 2))
                    act.wait_ge(gram_ready, 2 * STEPS * c + STEPS * h + s + 1)
                    last = act.copy(*product_views(h, s, 2))
                    last = act.copy(*product_views(h, s, 3))
                    last.then_inc(gram_act, 1)
                    if lookups and s < NL:
                        store_lookup(c, BASE, 1 - h, s)

            def mlp(c):
                for span in A_OF:
                    ps = take(c, BASE)
                    for i, a in enumerate(span):
                        n = NA - a
                        blk = ps[:, i * P:(i + 1) * P].rearrange("p (j b) -> p j b", j=QUAD)
                        last = act.copy(pairs[:, :, PAIR0[a]:PAIR0[a] + n], blk[:, :, a + 1:F])
                    last.then_inc(emptied, 1)
                act.wait_ge(y_stored, 16 * (c + 1))
                for k, (k0, w) in enumerate(K_PAIR):
                    ps = take(c, BASE)
                    act.copy(pairs_t[0:w, k, :], ps[0:w, :]).then_inc(emptied, 1)
                act.wait_ge(weights_landed, 16 * N_WEIGHTS)
                for n in range(H1 // P):
                    ps = take(c, BASE)
                    act.activation(h1[:, n, :], ps[:], ACT.Relu, bias=b1[:, n:n + 1]).then_inc(emptied, 1)
                for n in range(H2 // P):
                    ps = take(c, BASE)
                    act.activation(h2[:, n, :], ps[:], ACT.Relu, bias=b2[:, n:n + 1]).then_inc(emptied, 1)
                ps = take(c, BASE)
                act.copy(y_row[0:1, :].rearrange("o (i j) -> o j i", j=QUAD),
                         ps[0:1, :].rearrange("o (j i) -> o j i", j=QUAD)).then_inc(emptied, 1)
                act.wait_ge(emptied, c * USES + BASE + use[0])
                act.dma_start(out[bass.ds(c * CHUNK, CHUNK), :].rearrange("s o -> o s"), y_row[0:1, :]).then_inc(y_stored, 16)

            act.sem_inc(y_stored, 16)
            for t in range(0, NTILE, 4):
                ps = take(0, 0)
                act.copy(ids_t[:, t * P:(t + 4) * P], ps[0:NTAB, :]).then_inc(emptied, 1)
            for m in range(NL):
                act.wait_ge(raw_landed[m % 2], 16 * (m // 2 + 1))
                act.copy(table_hi[:, m], raw[:, m % 2]).then_inc(hi_ready, 1)
                if m >= 1:
                    store_lookup(0, 0, 0, m - 1)
            store_lookup(0, 0, 0, NL - 1)
            act.wait_ge(w1_ready, 1)
            act.wait_ge(lo_ready, NL)
            act.wait_ge(hi_ready, NL)
            with act.Fori(0, NCHUNK - 1) as c:
                use[0] = 0
                half(c, 0, True)
                half(c, 1, True)
                mlp(c)
            use[0] = 0
            half(NCHUNK - 1, 0, True)
            half(NCHUNK - 1, 1, False)
            mlp(NCHUNK - 1)
            act.wait_ge(y_stored, 16 * (NCHUNK + 1))

        @block.vector
        def _(dve):
            def one_hot(M, ready, free):
                dve.wait_ge(idb_ready, ready)
                if free is not None:
                    dve.wait_ge(filled, free)
                dve.tensor_tensor(onehot[:, M % 2], idb[0:VP, M % 2, 0:HALF].unsqueeze(1).to_broadcast([VP, KT, HALF]),
                                  vrow[:].unsqueeze(2).to_broadcast([VP, KT, HALF]), ALU.is_equal).then_inc(onehot_ready, 1)

            dve.memset(A[:], 0.0).then_inc(cleared, 1)
            for h in range(2):
                dve.memset(XT[h][:, :, F:QW], 0.0).then_inc(cleared, 1)
            dve.wait_ge(ids_landed, 16)
            dve.wait_ge(cleared, 1)
            dve.tensor_copy(ids_f[:], ids_all[:]).then_inc(ids_f_ready, 1)
            dve.wait_ge(const_ready, 3)
            dve.tensor_copy(ident_r[:], ident[:]).then_inc(ident_r_ready, 1)
            dve.tensor_copy(vrow[:], vrow_i[:]).then_inc(vrow_ready, 1)
            dve.wait_ge(vrow_ready, 1)
            for m in range(NL):
                dve.wait_ge(hi_ready, m + 1)
                dve.tensor_tensor(table_lo[:, m], raw[:, m % 2], table_hi[:, m].bitcast(F32), ALU.subtract).then_inc(lo_ready, 1)
                one_hot(m, m + 1, NTILE // 4 + m - 1 if m >= 2 else None)
            one_hot(NL, NL + 1, NTILE // 4 + NL - 1)
            dve.wait_ge(weights_landed, 16 * N_WEIGHTS)
            dve.tensor_tensor(w1_dense[:], w1_dense[:], w1_again[:], ALU.add).then_inc(w1_ready, 1)

            def half(c, h, lookups, last_half=False):
                for s in range(STEPS):
                    dve.wait_ge(gram_ready, 2 * STEPS * c + STEPS * h + s + 1)
                    dve.tensor_copy(*product_views(h, s, 0))
                    dve.tensor_copy(*product_views(h, s, 1)).then_inc(gram_dve, 1)
                    if lookups and s < NL and not (last_half and s == NL - 1):
                        M = (h + 1) * NL + s + 1
                        if s >= 1:
                            free = lookup_done(c, h, s - 1)
                        else:
                            free = c * USES + BASE + (USES_HALF if h else 0)
                        one_hot(M, 2 * NL * c + M + 1, free)

            dve.wait_ge(w1_ready, 1)
            dve.wait_ge(lo_ready, NL)
            dve.wait_ge(hi_ready, NL)
            with dve.Fori(0, NCHUNK - 1) as c:
                half(c, 0, True)
                half(c, 1, True)
            half(NCHUNK - 1, 0, True, last_half=True)
            half(NCHUNK - 1, 1, False)


N_WEIGHTS = 9


_OUTS = [((2048, 1), 'float32')]
_INS = (["r_dense_features", "ids"] + [f"tbl_{i}" for i in range(26)]
        + ["W_top1", "b_top1", "W_top2", "b_top2", "W_top3"])


def kernel(**inputs):
    import numpy as np
    import concourse.bacc as bacc
    from concourse import mybir as mb
    from concourse.bass_utils import run_bass_kernel_spmd

    nc = bacc.Bacc("TRN2", target_bir_lowering=False, num_devices=1)
    arrays, aps = {}, {}
    for name in _INS:
        a = np.ascontiguousarray(inputs[name])
        arrays[f"in_{name}"] = a
        aps[name] = nc.dram_tensor(f"in_{name}", a.shape, mb.dt.from_np(a.dtype), kind="ExternalInput").ap()
    shape, dtype = _OUTS[0]
    out = nc.dram_tensor("out_y", shape, mb.dt.from_np(np.dtype(dtype)), kind="ExternalOutput").ap()
    build(nc, aps, out)
    r = run_bass_kernel_spmd(nc, [arrays], core_ids=[0])
    return r.results[0]["out_y"]
```

```python
from contextlib import ExitStack

import concourse.bass as bass
from concourse import mybir

F32 = mybir.dt.float32
F32R = mybir.dt.float32r
I32 = mybir.dt.int32
U32 = mybir.dt.uint32
ALU = mybir.AluOpType
ACT = mybir.ActivationFunctionType

P = 128
LOOKUP_TABLES = [2, 5, 10, 12, 13, 14]


def build(nc, aps, out):
    ids = aps["ids"]
    B, NTAB = ids.shape
    D = aps["r_dense_features"].shape[1]
    assert D == P
    F = NTAB + 1
    H1 = aps["W_top1"].shape[1]
    H2 = aps["W_top2"].shape[1]
    PAIRS = F * (F - 1) // 2

    TILE = P
    HALF = 2 * TILE
    ROUND = 2 * HALF
    NROUND = B // ROUND - 1
    NTILE = B // TILE
    NL = len(LOOKUP_TABLES)
    GATHER_TABLES = [f for f in range(NTAB) if f not in LOOKUP_TABLES]
    NG = len(GATHER_TABLES)
    ROWS_PER_PART = aps[f"tbl_{LOOKUP_TABLES[0]}"].shape[0] // 125
    VP = 125
    KT = ROWS_PER_PART
    assert all(aps[f"tbl_{f}"].shape[0] == VP * KT for f in LOOKUP_TABLES)

    QUAD = 4
    QW = 32
    NA = F - 1
    GROUPS_STEP = 8
    STEPS = HALF // QUAD // GROUPS_STEP
    PER_BANK = 4
    K_PAIR = [(k, min(P, PAIRS - k)) for k in range(0, PAIRS, P)]
    T_BANKS = 8
    A_OF = [range(NA * b // T_BANKS, NA * (b + 1) // T_BANKS) for b in range(T_BANKS)]
    PAIR0 = [F * a - a * (a + 1) // 2 for a in range(F)]

    FEAT = [0] + [f + 1 for f in GATHER_TABLES]
    XGROUPS = [[0]] + [list(range(g, min(g + 4, len(FEAT)))) for g in range(1, len(FEAT), 4)]
    RING = 3
    USES_X = len(XGROUPS)
    USES_MLP = T_BANKS + len(K_PAIR) + H1 // P + H2 // P + 1
    USES_START = NTILE // 4 + NL + 1 + USES_X + 2 * USES_X + NL
    USES_ROUND = 4 * USES_X + 2 * NL + USES_MLP
    assert USES_ROUND % RING == 0 and NL <= STEPS and B % ROUND == 0 and NTILE % 4 == 0

    NRAW = NL // 2
    SPLIT_ORDER = [*range(NRAW, NL), *range(NRAW)]
    ROW_GROUPS_OF = [range(USES_X * i // (STEPS // 2), USES_X * (i + 1) // (STEPS // 2)) for i in range(STEPS // 2)]
    EARLY_ROWS_OF = [range(0) if m < NRAW else range(USES_X * (m - NRAW) // (NL - NRAW), USES_X * (m - NRAW + 1) // (NL - NRAW))
                     for m in range(NL)]

    START, FIRST, MIDDLE, LAST, END = range(5)
    TILES = {START: (2, 3), FIRST: (0, 1, 2, 3), MIDDLE: (0, 1, 2, 3), LAST: (0, 1)}
    BATCH = {FIRST: (0, P // 2), MIDDLE: (0, P), LAST: (0, P), END: (P // 2, P // 2)}
    PIECES = {(0, 1): ("layer1", 0), (0, 3): ("layer1", 1), (1, 1): ("layer1", 2), (1, 3): ("layer1", 3),
              (2, 1): ("layer2", 0), (2, 3): ("layer2", 1), (3, 1): ("layer3",)}
    LAST_PIECES = {(0, 0): ("layer1", 0), (0, 1): ("layer1", 1), (0, 2): ("layer1", 2), (0, 3): ("layer1", 3),
                   (1, 0): ("layer2", 0), (1, 1): ("layer2", 1), (1, 2): ("layer3",)}

    def stages(kind):
        if kind == END:
            yield "dense", *BATCH[END]
            for b in range(T_BANKS):
                yield "unblock", *BATCH[END], b
            for k in range(len(K_PAIR)):
                yield "pairs", *BATCH[END], k
            for n in range(H1 // P):
                yield "layer1", n
            for n in range(H2 // P):
                yield "layer2", n
            yield ("layer3",)
            return
        looks = kind != LAST
        for t in TILES[kind]:
            h, q = divmod(t, 2)
            if looks and q == 0:
                yield "spread", h, 0
            if t == 0:
                for b in range(T_BANKS):
                    yield "unblock", *BATCH[kind], b
            if t == 3:
                yield "dense", *BATCH[kind + 1 if kind != MIDDLE else MIDDLE]
            for i in range(STEPS // 2):
                s = q * (STEPS // 2) + i
                yield "products", h, s
                if t == 0 and i == 0:
                    yield "pairs", *BATCH[kind], 0
                if looks and s < NL:
                    yield "lookup", h, s
                if t == 0 and i == 0:
                    yield "pairs", *BATCH[kind], 1
                if looks or t == 0:
                    for g in ROW_GROUPS_OF[i]:
                        yield "rows", t + 1, g
                if t == 0 and i == 0:
                    yield "pairs", *BATCH[kind], 2
                if kind != START and (t, i) in (PIECES if looks else LAST_PIECES):
                    yield (PIECES if looks else LAST_PIECES)[t, i]

    def ring_start(r):
        return r * USES_ROUND + USES_START

    def bank_of(start, n):
        return ((USES_START if not isinstance(start, int) else start) + n) % RING

    def mlp_start(r):
        return r * USES_MLP

    def runs(slots):
        i = 0
        while i < len(slots):
            n = 1
            while i + n < len(slots) and slots[i + n] - slots[i + n - 1] == slots[min(i + 1, len(slots) - 1)] - slots[i]:
                n += 1
            yield i, slots[i], (slots[i + 1] - slots[i] if n > 1 else 1), n
            i += n

    with ExitStack() as ctx:
        def sb(name, shape, dt=F32):
            return ctx.enter_context(nc.sbuf_tensor(name, shape, dt))

        def sem(name):
            return ctx.enter_context(nc.semaphore(name))

        ident = sb("ident", [P, P])
        ident_r = sb("ident_r", [P, P], F32R)
        ids_t = sb("ids_t", [NTAB, B - HALF], F32R)
        ids_tile = sb("ids_tile", [P, 4, NTAB], I32)
        vrow_i = sb("vrow_i", [VP, KT], I32)
        vrow = sb("vrow", [VP, KT])
        table_hi = sb("table_hi", [VP, NL, KT, D], F32R)
        table_lo = sb("table_lo", [VP, NL, KT, D], F32R)
        onehot = sb("onehot", [VP, 2, KT, HALF], F32R)
        rows = sb("rows", [P, 2, 1 + NG, D])
        XT = [sb(f"xt{h}", [D, HALF, QW]) for h in range(2)]
        A = sb("A", [P, NA, P])
        pairs_or_h1 = sb("pairs_or_h1", [P, max(QUAD * PAIRS, H1 // P * ROUND)])
        pairs_t_or_h2 = sb("pairs_t_or_h2", [P, max(len(K_PAIR), H2 // P) * ROUND])
        dense_t = sb("dense_t", [D, ROUND])
        dense_mlp = sb("dense_mlp", [D, ROUND])
        w1_dense = sb("w1_dense", [D, H1])
        w1_pair = sb("w1_pair", [P, len(K_PAIR), H1])
        w2 = sb("w2", [P, H1 // P, H2])
        w3 = sb("w3", [P, H2 // P])
        b1 = sb("b1", [P, H1 // P])
        b2 = sb("b2", [P, H2 // P])

        pairs = pairs_or_h1[:, 0:QUAD * PAIRS].rearrange("p (j x) -> p j x", j=QUAD)
        h1 = pairs_or_h1[:, 0:H1 // P * ROUND].rearrange("p (n s) -> p n s", s=ROUND)
        pairs_t = pairs_t_or_h2[:, 0:len(K_PAIR) * ROUND].rearrange("p (k s) -> p k s", s=ROUND)
        h2 = pairs_t_or_h2[:, 0:H2 // P * ROUND].rearrange("p (n s) -> p n s", s=ROUND)
        y_row = pairs_t_or_h2[0:1, H2 // P * ROUND:(H2 // P + 1) * ROUND]
        early = XT[1][:].rearrange("d s f -> d (s f)")
        raw = early[0:VP, 0:NL * KT * D].rearrange("p (u k d) -> p u k d", u=NL, k=KT)
        ids_all = dense_t[:, 0:NTILE * NTAB].bitcast(I32).rearrange("p (t f) -> p t f", f=NTAB)
        w1_again = early[:, NL * KT * D:NL * KT * D + H1]
        ids_f = early[:, NL * KT * D + H1:NL * KT * D + H1 + NTILE * NTAB].rearrange("p (t f) -> p t f", f=NTAB)

        ring = ctx.enter_context(nc.psum_tensor("ring", [P, RING, 512], F32))
        idb = ctx.enter_context(nc.psum_tensor("idb", [P, HALF], F32))
        gram = ctx.enter_context(nc.psum_tensor("gram", [P, 2, 2, 512], F32))

        ids_landed = sem("ids_landed")
        ids_slot = [sem(f"ids_slot{t}") for t in range(4)]
        rows_landed = [sem(f"rows_landed{q}") for q in range(2)]
        dense_landed = [sem(f"dense_landed{q}") for q in range(2)]
        weights_landed = sem("weights_landed")
        raw_landed = [sem(f"raw_landed{u}") for u in range(NL)]
        const_ready = sem("const_ready")
        a_cleared = sem("a_cleared")
        xt1_free = sem("xt1_free")
        ids_f_ready = sem("ids_f_ready")
        ident_r_ready = sem("ident_r_ready")
        vrow_ready = sem("vrow_ready")
        hi_ready = sem("hi_ready")
        lo_ready = sem("lo_ready")
        w1_ready = sem("w1_ready")
        filled_ids = sem("filled_ids")
        filled_rows = sem("filled_rows")
        looked_up = sem("looked_up")
        filled_mlp = sem("filled_mlp")
        emptied = sem("emptied")
        idb_ready = sem("idb_ready")
        onehot_ready = sem("onehot_ready")
        gram_ready = sem("gram_ready")
        gram_act = sem("gram_act")
        gram_dve = sem("gram_dve")
        dense_kept = sem("dense_kept")
        y_stored = sem("y_stored")
        tiles_begun = sem("tiles_begun")
        block = ctx.enter_context(nc.Block())

        def product_views(h, s, j):
            g0 = ((1 - h) * STEPS + s) * GROUPS_STEP
            dst = A[QW * j:QW * j + F, :, g0:g0 + GROUPS_STEP].rearrange("b a (u g) -> b u g a", g=PER_BANK)
            src = gram[QW * j:QW * j + F, s % 2, :, 0:PER_BANK * QUAD * NA].rearrange(
                "b u (g x) -> b u g x", g=PER_BANK)[:, :, :, NA * j:NA * (j + 1)]
            return dst, src

        @block.sync
        def _(sp):
            def load_ids(r, t):
                src = ids[bass.ds(r * ROUND + (t + 2) * TILE, TILE), :]
                sp.dma_start(ids_tile[:, t, :], src).then_inc(ids_slot[t], 16)

            def load_dense(r, t):
                src = aps["r_dense_features"][bass.ds(r * ROUND + (t + 2) * TILE, TILE), :]
                sp.dma_start(rows[:, t % 2, 0, :], src).then_inc(dense_landed[t % 2], 16)

            def load_dense_after(r, t):
                sp.wait_ge(filled_rows, USES_X * (4 * r + t + 1))
                load_dense(r, t)

            load_ids(-1, 2)
            sp.dma_start(ids_all[:], ids.rearrange("(t p) f -> p t f", p=P)).then_inc(ids_landed, 16)
            load_ids(-1, 3)
            load_ids(0, 0)
            load_ids(0, 1)
            load_dense(-1, 2)
            load_dense(-1, 3)
            for j, f in enumerate(LOOKUP_TABLES):
                sp.dma_start(raw[:, j], aps[f"tbl_{f}"].rearrange("(p k) d -> p k d", k=KT)).then_inc(raw_landed[j], 16)
            W1, W2 = aps["W_top1"], aps["W_top2"]
            sp.dma_start(w1_dense[:], W1[0:D, :]).then_inc(weights_landed, 16)
            sp.dma_start(w1_again[:], W1[D + PAIRS:2 * D + PAIRS, :]).then_inc(weights_landed, 16)
            for k, (k0, w) in enumerate(K_PAIR):
                sp.dma_start(w1_pair[0:w, k, :], W1[D + k0:D + k0 + w, :]).then_inc(weights_landed, 16)
            sp.dma_start(w2[:], W2.rearrange("(k p) n -> p k n", p=P)).then_inc(weights_landed, 16)
            with nc.allow_non_contiguous_dma(reason="biases and W3: a few hundred single values, once"):
                sp.dma_start(w3[:], aps["W_top3"].rearrange("(k p) o -> p (k o)", p=P)).then_inc(weights_landed, 16)
                sp.dma_start(b1[:], aps["b_top1"].rearrange("(n p) -> p n", p=P)).then_inc(weights_landed, 16)
                sp.dma_start(b2[:], aps["b_top2"].rearrange("(n p) -> p n", p=P)).then_inc(weights_landed, 16)

            def next_ids(r, t):
                sp.wait_ge(rows_landed[t % 2], 16 * NG * (2 * r + t // 2 + 1))
                load_ids(*((r, t + 2) if t < 2 else (r + 1, t - 2)))

            with sp.Fori(0, NROUND) as r:
                for t in range(4):
                    load_dense_after(r, t)
                    next_ids(r, t)
            load_dense_after(NROUND, 0)
            load_dense_after(NROUND, 1)

        @block.gpsimd
        def _(pool):
            def gathers(r, t):
                pool.wait_ge(ids_slot[t], 16 * (r + t // 2 + 1))
                pool.sem_inc(tiles_begun, 1)
                for r, f in enumerate(GATHER_TABLES):
                    pool.indirect_dma_start(
                        rows[:, t % 2, 1 + r, :], None, aps[f"tbl_{f}"],
                        bass.IndirectOffsetOnAxis(ap=ids_tile[:, t, f:f + 1].bitcast(U32), axis=0),
                    ).then_inc(rows_landed[t % 2], 16)

            def gathers_after(r, t):
                pool.wait_ge(filled_rows, USES_X * (4 * r + t + 1))
                gathers(r, t)

            pool.iota(vrow_i[:], pattern=[[1, KT]], base=0, channel_multiplier=KT).then_inc(const_ready, 1)
            pool.memset(ident[:], 0.0).then_inc(const_ready, 1)
            pool.wait_ge(const_ready, 2)
            pool.affine_select(out=ident[:], in_=ident[:], compare_op=ALU.not_equal, fill=1.0, base=0,
                               pattern=[[-1, P]], channel_multiplier=1).then_inc(const_ready, 1)
            gathers(-1, 2)
            gathers(-1, 3)
            with pool.Fori(0, NROUND) as r:
                for t in range(4):
                    gathers_after(r, t)
            gathers_after(NROUND, 0)
            gathers_after(NROUND, 1)

        @block.tensor
        def _(pe):
            use = [0]

            def claim(start):
                n = use[0]
                use[0] += 1
                if not isinstance(start, int) or start + n >= RING:
                    pe.wait_ge(emptied, start + n - RING + 1)
                return ring[:, bank_of(start, n), :]

            def spread_ids(m, col):
                f = LOOKUP_TABLES[m]
                pe.matmul(idb[:, 0:HALF], ident_r[0:NTAB, f:f + 1].to_broadcast([NTAB, P]),
                          ids_t[:, col], start=True, stop=True).then_inc(idb_ready, 1)

            def lookup(start, buf, m, ready, col):
                ps = claim(start)
                pe.wait_ge(onehot_ready, ready)
                for k in range(KT):
                    for part in (table_hi, table_lo):
                        last = pe.matmul(ps[:, 0:HALF], part[:, m, k, :], onehot[:, buf, k, :],
                                         start=(k == 0 and part is table_hi), stop=(k == KT - 1 and part is table_lo))
                    if k == 0 and m + 1 < NL:
                        spread_ids(m + 1, col)
                last.then_inc(looked_up, 1)

            def lookup_raw(m, col):
                ps = claim(0)
                pe.wait_ge(raw_landed[m], 16)
                pe.wait_ge(onehot_ready, m + 1)
                for k in range(KT):
                    last = pe.matmul(ps[:, 0:HALF], raw[:, m, k, :], onehot[:, m % 2, k, :].bitcast(F32),
                                     start=(k == 0), stop=(k == KT - 1))
                    if k == 0 and m + 1 < NL:
                        spread_ids(m + 1, col)
                last.then_inc(looked_up, 1)

            def transpose_rows(r, start, t, g):
                q = t % 2
                if g == 0:
                    pe.wait_ge(dense_landed[q], 16 * (2 * r + t // 2 + 2))
                    pe.wait_ge(rows_landed[q], 16 * NG * (2 * r + t // 2 + 2))
                ps = claim(start)
                for i, row in enumerate(XGROUPS[g]):
                    last = pe.transpose(ps[:, i * P:(i + 1) * P], rows[:, q, row, :], ident[:])
                last.then_inc(filled_rows, 1)

            def products(r, h, s):
                n = STEPS * (2 * r + 1 + h) + s
                if not isinstance(n, int) or n >= 2:
                    pe.wait_ge(gram_act, n - 1)
                    pe.wait_ge(gram_dve, n - 1)
                for g in range(GROUPS_STEP):
                    s0 = (s * GROUPS_STEP + g) * QUAD
                    four = XT[1 - h][:, s0:s0 + QUAD, :].rearrange("d j f -> d (j f)")
                    cols = XT[1 - h][:, s0:s0 + QUAD, 0:NA]
                    col = (g % PER_BANK) * QUAD * NA
                    last = pe.matmul(gram[:, s % 2, g // PER_BANK, col:col + QUAD * NA], four, cols,
                                     start=True, stop=True)
                last.then_inc(gram_ready, 1)

            def unblock(halves, start, i0, ni, b):
                if b == 0:
                    pe.wait_ge(gram_act, STEPS * halves)
                    pe.wait_ge(gram_dve, STEPS * halves)
                ps = claim(start)
                for i, a in enumerate(A_OF[b]):
                    last = pe.transpose(ps[0:ni, i * P:(i + 1) * P], A[:, a, i0:i0 + ni], ident[:])
                last.then_inc(filled_mlp, 1)

            def transpose_pairs(start, after, ni, k):
                if k == 0:
                    pe.wait_ge(emptied, after)
                k0, w = K_PAIR[k]
                ps = claim(start)
                for j in range(QUAD):
                    last = pe.transpose(ps[0:w, j * ni:(j + 1) * ni], pairs[0:ni, j, k0:k0 + w], ident[0:ni, 0:ni])
                last.then_inc(filled_mlp, 1)

            def layer1(start, after, ncol, n):
                if n == 0:
                    pe.wait_ge(w1_ready, 1)
                    pe.wait_ge(weights_landed, 16 * N_WEIGHTS)
                    pe.wait_ge(emptied, after)
                ps = claim(start)
                cols = slice(n * P, (n + 1) * P)
                pe.matmul(ps[:, 0:ncol], w1_dense[:, cols], dense_mlp[:, 0:ncol], start=True, stop=False)
                for k, (k0, w) in enumerate(K_PAIR):
                    last = pe.matmul(ps[:, 0:ncol], w1_pair[0:w, k, cols], pairs_t[0:w, k, 0:ncol], start=False,
                                     stop=(k == len(K_PAIR) - 1))
                last.then_inc(filled_mlp, 1)

            def layer2(start, after, ncol, n):
                if n == 0:
                    pe.wait_ge(emptied, after)
                ps = claim(start)
                for k in range(H1 // P):
                    last = pe.matmul(ps[:, 0:ncol], w2[:, k, n * P:(n + 1) * P], h1[:, k, 0:ncol], start=(k == 0),
                                     stop=(k == H1 // P - 1))
                last.then_inc(filled_mlp, 1)

            def layer3(start, after, ncol):
                pe.wait_ge(emptied, after)
                ps = claim(start)
                for k in range(H2 // P):
                    last = pe.matmul(ps[0:1, 0:ncol], w3[:, k:k + 1], h2[:, k, 0:ncol], start=(k == 0),
                                     stop=(k == H2 // P - 1))
                last.then_inc(filled_mlp, 1)

            def play(r, kind, start):
                after = ncol = None
                tile_done = use[0]
                for stage, *arg in stages(kind):
                    if stage == "rows":
                        transpose_rows(r, start, *arg)
                        if arg[1] == USES_X - 1:
                            tile_done = use[0]
                    elif stage == "products":
                        if arg[1] % (STEPS // 2) == 0:
                            pe.wait_ge(emptied, start + tile_done)
                        products(r, *arg)
                    elif stage == "spread":
                        h, m = arg
                        spread_ids(m, bass.ds((2 * r + 1 + h) * HALF, HALF))
                    elif stage == "lookup":
                        h, m = arg
                        lookup(start, (h * NL + m) % 2, m, (2 * r + 2 + h) * NL + m + 1,
                               bass.ds((2 * r + 1 + h) * HALF, HALF))
                    elif stage == "unblock":
                        unblock(2 * r + 2 if kind == END else 2 * r + 1, start, *arg)
                        ncol, after = arg[1] * QUAD, start + use[0]
                    elif stage == "pairs":
                        i0, ni, k = arg
                        transpose_pairs(start, after, ni, k)
                        if k == len(K_PAIR) - 1:
                            after = start + use[0]
                    elif stage == "layer1":
                        layer1(start, after, ncol, *arg)
                        if arg[0] == H1 // P - 1:
                            after = start + use[0]
                    elif stage == "layer2":
                        layer2(start, after, ncol, *arg)
                        if arg[0] == H2 // P - 1:
                            after = start + use[0]
                    elif stage == "layer3":
                        layer3(start, after, ncol)

            def transpose_ids(t, n):
                ps = claim(0)
                for i in range(n):
                    last = pe.transpose(ps[0:NTAB, i * P:(i + 1) * P], ids_f[:, t + i, :], ident[:])
                last.then_inc(filled_ids, 1)

            pe.wait_ge(const_ready, 3)
            pe.wait_ge(ids_f_ready, 1)
            transpose_ids(0, 2)
            transpose_ids(2, 4)
            pe.wait_ge(emptied, 1)
            pe.wait_ge(ident_r_ready, 1)
            col = slice(B - 2 * HALF, B - HALF)
            spread_ids(0, col)
            for t in range(6, NTILE - 2, 4):
                transpose_ids(t, 4)
            for m in range(NL):
                if m < NRAW:
                    lookup_raw(m, col)
                else:
                    pe.wait_ge(hi_ready, m - NRAW + 1)
                    pe.wait_ge(lo_ready, m - NRAW + 1)
                    lookup(0, m % 2, m, m + 1, col)
                for g in EARLY_ROWS_OF[m]:
                    transpose_rows(-1, 0, 2, g)
            transpose_ids(NTILE - 2, 2)
            pe.wait_ge(hi_ready, NL)
            pe.wait_ge(lo_ready, NL)
            pe.wait_ge(a_cleared, 2)
            play(-1, START, 0)
            use[0] = 0
            play(0, FIRST, ring_start(0))
            with pe.Fori(1, NROUND) as r:
                use[0] = 0
                play(r, MIDDLE, ring_start(r))
            use[0] = 0
            play(NROUND, LAST, ring_start(NROUND))
            play(NROUND, END, ring_start(NROUND))

        @block.scalar
        def _(act):
            use = [0]
            mlp_use = [0]

            def bank(start):
                n = use[0]
                use[0] += 1
                return ring[:, bank_of(start, n), :]

            def store_lookup(start, h, m, ready):
                act.wait_ge(looked_up, ready)
                act.copy(XT[h][:, :, LOOKUP_TABLES[m] + 1], bank(start)[:, 0:HALF]).then_inc(emptied, 1)

            def store_rows(r, start, t, g):
                h, q = divmod((t + 2) % 4, 2)
                xt = XT[h][:, q * TILE:(q + 1) * TILE, :]
                act.wait_ge(filled_rows, USES_X * (4 * r + t + 2) + g + 1)
                ps = bank(start)
                for i, f0, step, n in runs([FEAT[row] for row in XGROUPS[g]]):
                    last = act.copy(xt[:, :, f0:f0 + step * (n - 1) + 1:step].rearrange("d s f -> d f s"),
                                    ps[:, i * P:(i + n) * P].rearrange("d (f s) -> d f s", f=n))
                if g == 0:
                    if t == 4:
                        act.wait_ge(dense_kept, r + 2)
                    w = TILE // QUAD
                    i0 = (2 * h + q) * w
                    last = act.copy(dense_t[:].rearrange("d (j i) -> d j i", j=QUAD)[:, :, i0:i0 + w],
                                    ps[:, 0:P].rearrange("d (i j) -> d j i", j=QUAD))
                last.then_inc(emptied, 1)

            def store_products(r, h, s):
                act.wait_ge(gram_ready, STEPS * (2 * r + 1 + h) + s + 1)
                act.copy(*product_views(h, s, 2))
                act.copy(*product_views(h, s, 3)).then_inc(gram_act, 1)

            def keep_dense(start, i0, ni):
                act.wait_ge(emptied, start + use[0])
                act.copy(dense_mlp[:, 0:QUAD * ni].rearrange("d (j i) -> d j i", j=QUAD),
                         dense_t[:].rearrange("d (j i) -> d j i", j=QUAD)[:, :, i0:i0 + ni]).then_inc(dense_kept, 1)

            def mlp_bank(start, mlp0):
                act.wait_ge(filled_mlp, mlp0 + mlp_use[0] + 1)
                mlp_use[0] += 1
                return bank(start)

            def store_unblocked(start, mlp0, i0, ni, b):
                ps = mlp_bank(start, mlp0)
                for i, a in enumerate(A_OF[b]):
                    n = NA - a
                    blk = ps[0:ni, i * P:(i + 1) * P].rearrange("p (j b) -> p j b", j=QUAD)
                    last = act.copy(pairs[0:ni, :, PAIR0[a]:PAIR0[a] + n], blk[:, :, a + 1:F])
                last.then_inc(emptied, 1)

            def store_pairs(start, mlp0, stores, i0, ni, k):
                if k == 0 and stores is not None:
                    act.wait_ge(y_stored, 16 * stores)
                k0, w = K_PAIR[k]
                ps = mlp_bank(start, mlp0)
                act.copy(pairs_t[0:w, k, 0:QUAD * ni], ps[0:w, 0:QUAD * ni]).then_inc(emptied, 1)

            def store_layer(start, mlp0, h_next, bias, ncol, n):
                act.wait_ge(weights_landed, 16 * N_WEIGHTS)
                ps = mlp_bank(start, mlp0)
                act.activation(h_next[:, n, 0:ncol], ps[:, 0:ncol], ACT.Relu, bias=bias[:, n:n + 1]).then_inc(emptied, 1)

            def store_y(r, start, mlp0, kind):
                i0, ni = BATCH[kind]
                ps = mlp_bank(start, mlp0)
                act.copy(y_row[0:1, 0:QUAD * ni].rearrange("o (i j) -> o j i", j=QUAD),
                         ps[0:1, 0:QUAD * ni].rearrange("o (j i) -> o j i", j=QUAD)).then_inc(emptied, 1)
                act.wait_ge(emptied, start + use[0])
                for i in range(i0, i0 + ni, P // 2):
                    first = r * ROUND + (HALF if kind == END else 0 if i == 0 else -HALF)
                    y = y_row[0:1, QUAD * (i - i0):QUAD * (i - i0) + HALF]
                    act.dma_start(out[bass.ds(first, HALF), :].rearrange("s o -> o s"), y).then_inc(y_stored, 16)

            def play(r, kind, start, mlp0, stores):
                ncol = kind != START and QUAD * BATCH[kind][1]
                for stage, *arg in stages(kind):
                    if stage == "rows":
                        store_rows(r, start, *arg)
                    elif stage == "products":
                        store_products(r, *arg)
                    elif stage == "lookup":
                        h, m = arg
                        store_lookup(start, h, m, (2 * r + 2 + h) * NL + m + 1)
                    elif stage == "dense":
                        keep_dense(start, *arg)
                    elif stage == "unblock":
                        store_unblocked(start, mlp0, *arg)
                    elif stage == "pairs":
                        store_pairs(start, mlp0, stores, *arg)
                    elif stage == "layer1":
                        store_layer(start, mlp0, h1, b1, ncol, *arg)
                    elif stage == "layer2":
                        store_layer(start, mlp0, h2, b2, ncol, *arg)
                    elif stage == "layer3":
                        store_y(r, start, mlp0, kind)

            def store_ids(col, n, ready):
                act.wait_ge(filled_ids, ready)
                act.copy(ids_t[:, col:col + n], bank(0)[0:NTAB, 0:n]).then_inc(emptied, 1)

            store_ids(B - 2 * HALF, HALF, 1)
            for t in range(2, NTILE - 2, 4):
                store_ids((t - 2) * P, 4 * P, (t + 2) // 4 + 1)
            n_split = 0
            for m in range(NL):
                for j in SPLIT_ORDER[n_split:(m + 1) * (NL // 2 + 1)]:
                    act.wait_ge(raw_landed[j], 16)
                    act.copy(table_hi[:, j], raw[:, j]).then_inc(hi_ready, 1)
                    n_split += 1
                store_lookup(0, 0, m, m + 1)
                for g in EARLY_ROWS_OF[m]:
                    store_rows(-1, 0, 2, g)
            store_ids(B - 2 * HALF, HALF, NTILE // 4 + 1)
            act.wait_ge(xt1_free, 1)
            play(-1, START, 0, 0, None)
            use[0] = mlp_use[0] = 0
            play(0, FIRST, ring_start(0), mlp_start(0), None)
            with act.Fori(1, NROUND) as r:
                use[0] = mlp_use[0] = 0
                play(r, MIDDLE, ring_start(r), mlp_start(r), 2 * r - 1)
            use[0] = mlp_use[0] = 0
            play(NROUND, LAST, ring_start(NROUND), mlp_start(NROUND), 2 * NROUND - 1)
            play(NROUND, END, ring_start(NROUND), mlp_start(NROUND), 2 * NROUND + 1)
            act.wait_ge(y_stored, 16 * (2 * NROUND + 2))

        @block.vector
        def _(dve):
            def one_hot(buf, ready, free):
                dve.wait_ge(idb_ready, ready)
                if free is not None:
                    dve.wait_ge(looked_up, free)
                dve.tensor_tensor(onehot[:, buf], idb[0:VP, 0:HALF].unsqueeze(1).to_broadcast([VP, KT, HALF]),
                                  vrow[:].unsqueeze(2).to_broadcast([VP, KT, HALF]), ALU.is_equal).then_inc(onehot_ready, 1)

            def lower_part(n):
                m = SPLIT_ORDER[n]
                dve.wait_ge(hi_ready, n + 1)
                dve.tensor_tensor(table_lo[:, m], raw[:, m], table_hi[:, m].bitcast(F32), ALU.subtract).then_inc(lo_ready, 1)

            dve.memset(A[:], 0.0).then_inc(a_cleared, 1)
            dve.wait_ge(ids_landed, 16)
            dve.tensor_copy(ids_f[:], ids_all[:]).then_inc(ids_f_ready, 1)
            dve.wait_ge(const_ready, 3)
            dve.tensor_copy(ident_r[:], ident[:]).then_inc(ident_r_ready, 1)
            dve.tensor_copy(vrow[:], vrow_i[:]).then_inc(vrow_ready, 1)
            dve.memset(XT[0][:, :, F:QW], 0.0).then_inc(a_cleared, 1)
            dve.wait_ge(vrow_ready, 1)
            for m in range(NL):
                if m >= NRAW:
                    lower_part(m - NRAW)
                one_hot(m % 2, m + 1, m - 1 if m >= 2 else None)
            for n in range(NL - NRAW, NL):
                lower_part(n)
            dve.wait_ge(weights_landed, 16 * N_WEIGHTS)
            dve.tensor_tensor(w1_dense[:], w1_dense[:], w1_again[:], ALU.add).then_inc(w1_ready, 1)
            dve.wait_ge(lo_ready, NL)
            dve.wait_ge(looked_up, NRAW)
            dve.wait_ge(w1_ready, 1)
            dve.wait_ge(filled_ids, NTILE // 4 + 1)
            dve.memset(XT[1][:, :, F:QW], 0.0).then_inc(xt1_free, 1)

            def play(r, kind):
                for stage, *arg in stages(kind):
                    if stage == "products":
                        h, s = arg
                        dve.wait_ge(gram_ready, STEPS * (2 * r + 1 + h) + s + 1)
                        dve.tensor_copy(*product_views(h, s, 0))
                        dve.tensor_copy(*product_views(h, s, 1)).then_inc(gram_dve, 1)
                    elif stage == "spread" or stage == "lookup" and arg[1] + 1 < NL:
                        h, m = arg
                        if stage == "lookup":
                            m += 1
                        n = (2 * r + 2 + h) * NL + m
                        one_hot((h * NL + m) % 2, n + 1, n - 1)

            play(-1, START)
            play(0, FIRST)
            with dve.Fori(1, NROUND) as r:
                play(r, MIDDLE)
            play(NROUND, LAST)


N_WEIGHTS = 9


_OUTS = [((2048, 1), 'float32')]
_INS = (["r_dense_features", "ids"] + [f"tbl_{i}" for i in range(26)]
        + ["W_top1", "b_top1", "W_top2", "b_top2", "W_top3"])


def kernel(**inputs):
    import numpy as np
    import concourse.bacc as bacc
    from concourse import mybir as mb
    from concourse.bass_utils import run_bass_kernel_spmd

    nc = bacc.Bacc("TRN2", target_bir_lowering=False, num_devices=1)
    arrays, aps = {}, {}
    for name in _INS:
        a = np.ascontiguousarray(inputs[name])
        arrays[f"in_{name}"] = a
        aps[name] = nc.dram_tensor(f"in_{name}", a.shape, mb.dt.from_np(a.dtype), kind="ExternalInput").ap()
    shape, dtype = _OUTS[0]
    out = nc.dram_tensor("out_y", shape, mb.dt.from_np(np.dtype(dtype)), kind="ExternalOutput").ap()
    build(nc, aps, out)
    r = run_bass_kernel_spmd(nc, [arrays], core_ids=[0])
    return r.results[0]["out_y"]
```

```python
from contextlib import ExitStack

import concourse.bass as bass
from concourse import mybir

F32 = mybir.dt.float32
F32R = mybir.dt.float32r
I32 = mybir.dt.int32
U32 = mybir.dt.uint32
ALU = mybir.AluOpType
ACT = mybir.ActivationFunctionType

P = 128
LOOKUP_TABLES = [2, 5, 10, 12, 13, 14]


def build(nc, aps, out):
    ids = aps["ids"]
    B, NTAB = ids.shape
    D = aps["r_dense_features"].shape[1]
    assert D == P
    F = NTAB + 1
    H1 = aps["W_top1"].shape[1]
    H2 = aps["W_top2"].shape[1]
    PAIRS = F * (F - 1) // 2

    TILE = P
    HALF = 2 * TILE
    ROUND = 2 * HALF
    NROUND = B // ROUND - 1
    NTILE = B // TILE
    NL = len(LOOKUP_TABLES)
    GATHER_TABLES = [f for f in range(NTAB) if f not in LOOKUP_TABLES]
    NG = len(GATHER_TABLES)
    VP = 125
    KT = aps[f"tbl_{LOOKUP_TABLES[0]}"].shape[0] // VP
    assert all(aps[f"tbl_{f}"].shape[0] == VP * KT for f in LOOKUP_TABLES)

    QUAD = 4
    NI = HALF // QUAD
    QW = 32
    NA = F - 1
    GROUPS_STEP = 8
    STEPS = NI // GROUPS_STEP
    PER_BANK = 4
    K_PAIR = [(k, min(P, PAIRS - k)) for k in range(0, PAIRS, P)]
    NB1 = 1 + len(K_PAIR)
    assert H1 // P == NB1
    T_BANKS = 5
    COUPLES_OF = [range(NA // 2 * b // T_BANKS, NA // 2 * (b + 1) // T_BANKS) for b in range(T_BANKS)]
    PAIR0 = [F * a - a * (a + 1) // 2 for a in range(F)]

    FEAT = [0] + [f + 1 for f in GATHER_TABLES]
    XGROUPS = [[0]] + [list(range(g, min(g + 4, len(FEAT)))) for g in range(1, len(FEAT), 4)]
    RING = 3
    USES_X = len(XGROUPS)
    USES_MLP = T_BANKS + len(K_PAIR) + H1 // P + H2 // P + 1
    USES_START = NTILE // 4 + 1 + NL + USES_X + 2 * USES_X + NL
    USES_ROUND = 4 * USES_X + 2 * NL + 2 * USES_MLP
    assert USES_ROUND % RING == 0 and NL <= STEPS and B % ROUND == 0 and NTILE % 4 == 0

    NRAW = 2
    SPLIT_ORDER = [*range(NRAW, NL), *range(NRAW)]
    EARLY_ROWS_OF = [range(0)] * (NL - 2) + [range(USES_X // 2), range(USES_X // 2, USES_X)]
    WARM_UP = 16
    START, WHOLE, LAST, END = range(4)
    TILES = {START: (2, 3), WHOLE: (0, 1, 2, 3), LAST: (0, 1)}
    PIECES = {1: ("layer1", 0), 2: ("layer1", 1), 3: ("layer1", 2), 4: ("layer1", 3),
              5: ("layer2", 0), 6: ("layer2", 1), 7: ("layer3", 0)}
    assert [n for layer, n in PIECES.values()] == [*range(H1 // P), *range(H2 // P), 0] and max(PIECES) < STEPS
    LOOKUP_AFTER = {START: {s: s for s in range(NL)}, WHOLE: dict(zip((0, 2, 3, 5, 6, 7), range(NL))), LAST: {}}
    assert len(LOOKUP_AFTER[WHOLE]) == NL
    RING_STAGES = ("rows", "lookup", "unblock", "pairs", "layer1", "layer2", "layer3")

    def stages(kind):
        if kind == END:
            yield "dense", 1, 0
            for b in range(T_BANKS):
                yield "unblock", 1, b
            for k in range(len(K_PAIR)):
                yield "pairs", 1, k
            for layer, n in PIECES.values():
                yield layer, 1, n
            return
        for t in TILES[kind]:
            h, q = divmod(t, 2)
            if q == 0 and kind != START:
                yield "dense", h, 0
            if q == 0 and kind != LAST:
                yield "spread", h, 0
            if q == 0 and kind != START:
                for b in range(T_BANKS):
                    yield "unblock", h, b
            if q == 1 and kind == START:
                yield "leftovers", h, 0
            for s in range(q * STEPS // 2, (q + 1) * STEPS // 2):
                piece = [(PIECES[s][0], h, PIECES[s][1])] if s in PIECES and kind != START else []
                yield "products", h, s
                if s == STEPS - 1:
                    yield from piece
                if s in LOOKUP_AFTER[kind]:
                    yield "lookup", h, LOOKUP_AFTER[kind][s]
                if s == 0 and kind != START:
                    for k in range(len(K_PAIR)):
                        yield "pairs", h, k
                if s % (STEPS // 2) == STEPS // 2 - 1 and (kind, t) != (LAST, 1):
                    for g in range(USES_X):
                        yield "rows", t + 1, g
                if s < STEPS - 1:
                    yield from piece

    def ring_start(r):
        return r * USES_ROUND + USES_START

    def bank_of(start, n):
        return ((USES_START if not isinstance(start, int) else start) + n) % RING

    def mlp_start(r):
        return 2 * r * USES_MLP

    def runs(slots):
        i = 0
        while i < len(slots):
            n = 1
            while i + n < len(slots) and slots[i + n] - slots[i + n - 1] == slots[min(i + 1, len(slots) - 1)] - slots[i]:
                n += 1
            yield i, slots[i], (slots[i + 1] - slots[i] if n > 1 else 1), n
            i += n

    with ExitStack() as ctx:
        def sb(name, shape, dt=F32):
            return ctx.enter_context(nc.sbuf_tensor(name, shape, dt))

        def sem(name):
            return ctx.enter_context(nc.semaphore(name))

        ident = sb("ident", [P, P])
        ident_r = sb("ident_r", [P, P], F32R)
        ids_t = sb("ids_t", [NTAB, B - HALF], F32R)
        ids_tile = sb("ids_tile", [P, 4, NTAB], I32)
        vrow_i = sb("vrow_i", [VP, KT], I32)
        vrow = sb("vrow", [VP, KT])
        table_hi = sb("table_hi", [VP, NL, KT, D], F32R)
        table_lo = sb("table_lo", [VP, NL, KT, D], F32R)
        onehot = sb("onehot", [VP, 2, KT, HALF], F32R)
        rows = sb("rows", [P, 2, 1 + NG, D])
        XT = [sb(f"xt{h}", [D, HALF, QW]) for h in range(2)]
        A = sb("A", [P, NA, NI])
        pairs_or_h1 = sb("pairs_or_h1", [P, max(QUAD * PAIRS, H1 // P * HALF)])
        pairs_t_or_h2 = sb("pairs_t_or_h2", [P, max(len(K_PAIR), H2 // P + 1) * HALF])
        x_or_h1_split = sb("x_or_h1_split", [P, 2, NB1, HALF], F32R)
        w1 = [sb(f"w1_{part}", [P, NB1, H1], F32R) for part in ("hi", "lo")]
        w2 = [sb(f"w2_{part}", [P, H1 // P, H2], F32R) for part in ("hi", "lo")]
        w3 = sb("w3", [P, H2 // P])
        b1 = sb("b1", [P, H1 // P])
        b2 = sb("b2", [P, H2 // P])

        pairs = pairs_or_h1[0:NI, 0:QUAD * PAIRS].rearrange("p (j x) -> p j x", j=QUAD)
        h1 = pairs_or_h1[:, 0:H1 // P * HALF].rearrange("p (n s) -> p n s", s=HALF)
        pairs_t = pairs_t_or_h2[:, 0:len(K_PAIR) * HALF].rearrange("p (k s) -> p k s", s=HALF)
        h2 = pairs_t_or_h2[:, 0:H2 // P * HALF].rearrange("p (n s) -> p n s", s=HALF)
        y_row = pairs_t_or_h2[0:1, H2 // P * HALF:(H2 // P + 1) * HALF]
        x_split = [x_or_h1_split[:, part] for part in range(2)]
        h1_split = x_split
        early = XT[1][:].rearrange("d s f -> d (s f)")
        raw = early[0:VP, 0:NL * KT * D].rearrange("p (u k d) -> p u k d", u=NL, k=KT)
        w1_pair_raw = early[:, NL * KT * D:NL * KT * D + len(K_PAIR) * H1].rearrange("p (k n) -> p k n", n=H1)
        early_a = A[:].rearrange("p a g -> p (a g)")
        w1_dense_raw = early_a[:, 0:H1]
        w1_again = early_a[:, H1:2 * H1]
        ids_f = early_a[:, 2 * H1:2 * H1 + NTILE * NTAB].rearrange("p (t f) -> p t f", f=NTAB)
        ids_all = pairs_t_or_h2[:, 0:NTILE * NTAB].bitcast(I32).rearrange("p (t f) -> p t f", f=NTAB)
        w2_raw = pairs_or_h1[:, 0:H1 // P * H2].rearrange("p (k n) -> p k n", n=H2)

        ring = ctx.enter_context(nc.psum_tensor("ring", [P, RING, 512], F32))
        idb = ctx.enter_context(nc.psum_tensor("idb", [P, HALF], F32))
        gram = ctx.enter_context(nc.psum_tensor("gram", [P, 2, 2, 512], F32))

        ids_landed = sem("ids_landed")
        ids_slot = [sem(f"ids_slot{t}") for t in range(4)]
        rows_landed = [sem(f"rows_landed{q}") for q in range(2)]
        dense_landed = [sem(f"dense_landed{q}") for q in range(2)]
        weights_landed = sem("weights_landed")
        raw_landed = [sem(f"raw_landed{u}") for u in range(NL)]
        const_ready = sem("const_ready")
        xt0_cleared = sem("xt0_cleared")
        xt1_cleared = sem("xt1_cleared")
        places_free = sem("places_free")
        ids_f_ready = sem("ids_f_ready")
        ident_r_ready = sem("ident_r_ready")
        vrow_ready = sem("vrow_ready")
        hi_ready = sem("hi_ready")
        lo_ready = sem("lo_ready")
        w1_ready = sem("w1_ready")
        filled_ids = sem("filled_ids")
        filled_rows = sem("filled_rows")
        looked_up = sem("looked_up")
        filled_mlp = sem("filled_mlp")
        emptied = sem("emptied")
        idb_ready = sem("idb_ready")
        onehot_ready = sem("onehot_ready")
        gram_ready = sem("gram_ready")
        gram_act = sem("gram_act")
        gram_dve = sem("gram_dve")
        weights_hi = sem("weights_hi")
        weights_lo = sem("weights_lo")
        dense_hi = sem("dense_hi")
        dense_lo = sem("dense_lo")
        pairs_lo = sem("pairs_lo")
        h1_hi = sem("h1_hi")
        h1_lo = sem("h1_lo")
        y_stored = sem("y_stored")
        tiles_begun = sem("tiles_begun")
        pairs_begun = sem("pairs_begun")
        block = ctx.enter_context(nc.Block())

        def product_views(s, j):
            g0 = s * GROUPS_STEP
            dst = A[QW * j:QW * (j + 1), :, g0:g0 + GROUPS_STEP].rearrange("b a (u g) -> b u g a", g=PER_BANK)
            src = gram[QW * j:QW * (j + 1), s % 2, :, 0:PER_BANK * QUAD * NA].rearrange(
                "b u (g x) -> b u g x", g=PER_BANK)[:, :, :, NA * j:NA * (j + 1)]
            return dst, src

        def weight_parts(w1_part, w2_part):
            k, w = len(K_PAIR), K_PAIR[-1][1]
            return [(w1_part[:, 1:k], w1_pair_raw[:, 0:k - 1]), (w1_part[0:w, k], w1_pair_raw[0:w, k - 1]),
                    (w1_part[:, 0], w1_dense_raw), (w2_part[:], w2_raw)]

        @block.sync
        def _(sp):
            def load_ids(r, t):
                src = ids[bass.ds(r * ROUND + (t + 2) * TILE, TILE), :]
                sp.dma_start(ids_tile[:, t, :], src).then_inc(ids_slot[t], 16)

            def load_dense(r, t):
                src = aps["r_dense_features"][bass.ds(r * ROUND + (t + 2) * TILE, TILE), :]
                sp.dma_start(rows[:, t % 2, 0, :], src).then_inc(dense_landed[t % 2], 16)

            def load_dense_after(r, t):
                sp.wait_ge(filled_rows, USES_X * (4 * r + t + 1))
                load_dense(r, t)

            load_ids(-1, 2)
            sp.dma_start(ids_all[:], ids.rearrange("(t p) f -> p t f", p=P)).then_inc(ids_landed, 16)
            load_ids(-1, 3)
            load_ids(0, 0)
            load_ids(0, 1)
            load_dense(-1, 2)
            load_dense(-1, 3)
            for j, f in enumerate(LOOKUP_TABLES):
                sp.dma_start(raw[:, j], aps[f"tbl_{f}"].rearrange("(p k) d -> p k d", k=KT)).then_inc(raw_landed[j], 16)
            W1, W2 = aps["W_top1"], aps["W_top2"]
            sp.dma_start(w1_dense_raw, W1[0:D, :]).then_inc(weights_landed, 16)
            sp.dma_start(w1_again, W1[D + PAIRS:2 * D + PAIRS, :]).then_inc(weights_landed, 16)
            for k, (k0, w) in enumerate(K_PAIR):
                sp.dma_start(w1_pair_raw[0:w, k, :], W1[D + k0:D + k0 + w, :]).then_inc(weights_landed, 16)
            sp.dma_start(w2_raw[:], W2.rearrange("(k p) n -> p k n", p=P)).then_inc(weights_landed, 16)
            with nc.allow_non_contiguous_dma(reason="biases and W3: a few hundred single values, once"):
                sp.dma_start(w3[:], aps["W_top3"].rearrange("(k p) o -> p (k o)", p=P)).then_inc(weights_landed, 16)
                sp.dma_start(b1[:], aps["b_top1"].rearrange("(n p) -> p n", p=P)).then_inc(weights_landed, 16)
                sp.dma_start(b2[:], aps["b_top2"].rearrange("(n p) -> p n", p=P)).then_inc(weights_landed, 16)

            def next_ids(r, t):
                sp.wait_ge(rows_landed[t % 2], 16 * NG * (2 * r + t // 2 + 1))
                load_ids(*((r, t + 2) if t < 2 else (r + 1, t - 2)))

            with sp.Fori(0, NROUND) as r:
                for t in range(4):
                    load_dense_after(r, t)
                    next_ids(r, t)
            load_dense_after(NROUND, 0)
            load_dense_after(NROUND, 1)

        @block.gpsimd
        def _(pool):
            def gathers(r, t):
                pool.wait_ge(ids_slot[t], 16 * (r + t // 2 + 1))
                pool.sem_inc(tiles_begun, 1)
                for r, f in enumerate(GATHER_TABLES):
                    pool.indirect_dma_start(
                        rows[:, t % 2, 1 + r, :], None, aps[f"tbl_{f}"],
                        bass.IndirectOffsetOnAxis(ap=ids_tile[:, t, f:f + 1].bitcast(U32), axis=0),
                    ).then_inc(rows_landed[t % 2], 16)

            def gathers_after(r, t):
                pool.wait_ge(filled_rows, USES_X * (4 * r + t + 1))
                gathers(r, t)

            pool.iota(vrow_i[:], pattern=[[1, KT]], base=0, channel_multiplier=KT).then_inc(const_ready, 1)
            pool.memset(ident[:], 0.0).then_inc(const_ready, 1)
            pool.wait_ge(const_ready, 2)
            pool.affine_select(out=ident[:], in_=ident[:], compare_op=ALU.not_equal, fill=1.0, base=0,
                               pattern=[[-1, P]], channel_multiplier=1).then_inc(const_ready, 1)
            gathers(-1, 2)
            gathers(-1, 3)
            with pool.Fori(0, NROUND) as r:
                for t in range(4):
                    gathers_after(r, t)
            gathers_after(NROUND, 0)
            gathers_after(NROUND, 1)

        @block.tensor
        def _(pe):
            use = [0]

            def claim(start):
                n = use[0]
                use[0] += 1
                if not isinstance(start, int) or start + n >= RING:
                    pe.wait_ge(emptied, start + n - RING + 1)
                return ring[:, bank_of(start, n), :]

            def spread_ids(m, col):
                f = LOOKUP_TABLES[m]
                pe.matmul(idb[:, 0:HALF], ident_r[0:NTAB, f:f + 1].to_broadcast([NTAB, P]),
                          ids_t[:, col], start=True, stop=True).then_inc(idb_ready, 1)

            def lookup(start, buf, m, ready, col):
                ps = claim(start)
                pe.wait_ge(onehot_ready, ready)
                for k in range(KT):
                    for part in (table_hi, table_lo):
                        last = pe.matmul(ps[:, 0:HALF], part[:, m, k, :], onehot[:, buf, k, :],
                                         start=(k == 0 and part is table_hi), stop=(k == KT - 1 and part is table_lo))
                    if k == 0 and m + 1 < NL:
                        spread_ids(m + 1, col)
                last.then_inc(looked_up, 1)

            def lookup_raw(m, col):
                ps = claim(0)
                pe.wait_ge(raw_landed[m], 16)
                pe.wait_ge(onehot_ready, m + 1)
                for k in range(KT):
                    last = pe.matmul(ps[:, 0:HALF], raw[:, m, k, :], onehot[:, m % 2, k, :].bitcast(F32),
                                     start=(k == 0), stop=(k == KT - 1))
                    if k == 0 and m + 1 < NL:
                        spread_ids(m + 1, col)
                last.then_inc(looked_up, 1)

            def transpose_rows(r, start, t, g):
                q = t % 2
                if g == 0:
                    pe.wait_ge(dense_landed[q], 16 * (2 * r + t // 2 + 2))
                    pe.wait_ge(rows_landed[q], 16 * NG * (2 * r + t // 2 + 2))
                ps = claim(start)
                for i, row in enumerate(XGROUPS[g]):
                    last = pe.transpose(ps[:, i * P:(i + 1) * P], rows[:, q, row, :], ident[:])
                last.then_inc(filled_rows, 1)

            def products(r, h, s):
                n = STEPS * (2 * r + 1 + h) + s
                if not isinstance(n, int) or n >= 2:
                    pe.wait_ge(gram_act, n - 1)
                    pe.wait_ge(gram_dve, n - 1)
                for g in range(GROUPS_STEP):
                    s0 = (s * GROUPS_STEP + g) * QUAD
                    four = XT[1 - h][:, s0:s0 + QUAD, :].rearrange("d j f -> d (j f)")
                    cols = XT[1 - h][:, s0:s0 + QUAD, 0:NA]
                    col = (g % PER_BANK) * QUAD * NA
                    last = pe.matmul(gram[:, s % 2, g // PER_BANK, col:col + QUAD * NA], four, cols,
                                     start=True, stop=True)
                last.then_inc(gram_ready, 1)

            def unblock(H, start, b):
                if b == 0:
                    pe.wait_ge(gram_act, STEPS * H)
                    pe.wait_ge(gram_dve, STEPS * H)
                ps = claim(start)
                for i, u in enumerate(COUPLES_OF[b]):
                    couple = A[:, 2 * u:2 * u + 2, :].rearrange("p a g -> p (a g)")
                    last = pe.transpose(ps[:, i * P:(i + 1) * P], couple, ident[:])
                last.then_inc(filled_mlp, 1)

            def transpose_pairs(start, after, k):
                if k == 0:
                    pe.wait_ge(emptied, after)
                k0, w = K_PAIR[k]
                ps = claim(start)
                pe.sem_inc(pairs_begun, 1)
                for j in range(QUAD):
                    last = pe.transpose(ps[0:w, j * NI:(j + 1) * NI], pairs[:, j, k0:k0 + w], ident[0:NI, 0:NI])
                last.then_inc(filled_mlp, 1)

            def split_products(ps, blocks, w, x, ready):
                terms = [(k, rows, wp, xp) for k, rows in blocks for wp, xp in ((0, 0), (1, 0), (0, 1))]
                for i, (k, rows, wp, xp) in enumerate(terms):
                    if ready is not None and i % 3 == 0:
                        pe.wait_ge(*ready[k])
                    last = pe.matmul(ps, w[wp][0:rows, k], x[xp][0:rows, k, :], start=(i == 0), stop=(i == len(terms) - 1))
                last.then_inc(filled_mlp, 1)

            def layer1(H, start, n):
                if n == 0:
                    pe.wait_ge(weights_lo, WEIGHT_PARTS)
                ready = [(dense_lo, H)] + [(pairs_lo, len(K_PAIR) * (H - 1) + k + 1) for k in range(len(K_PAIR))]
                w = [part[:, :, n * P:(n + 1) * P] for part in w1]
                blocks = [(0, D)] + [(1 + k, width) for k, (k0, width) in enumerate(K_PAIR)]
                split_products(claim(start)[:, 0:HALF], blocks, w, x_split, ready if n == 0 else None)

            def layer2(H, start, n):
                ready = [(h1_lo, H1 // P * (H - 1) + k + 1) for k in range(H1 // P)]
                w = [part[:, :, n * P:(n + 1) * P] for part in w2]
                split_products(claim(start)[:, 0:HALF], [(k, P) for k in range(H1 // P)], w, h1_split,
                               ready if n == 0 else None)

            def layer3(start, after):
                pe.wait_ge(emptied, after)
                ps = claim(start)
                for k in range(H2 // P):
                    last = pe.matmul(ps[0:1, 0:HALF], w3[:, k:k + 1], h2[:, k, :], start=(k == 0),
                                     stop=(k == H2 // P - 1))
                last.then_inc(filled_mlp, 1)

            def play(r, kind, start):
                after = None
                tile_done = use[0]
                for stage, *arg in stages(kind):
                    if stage == "rows":
                        transpose_rows(r, start, *arg)
                        if arg[1] == USES_X - 1:
                            tile_done = use[0]
                    elif stage == "products":
                        if arg[1] % (STEPS // 2) == 0:
                            pe.wait_ge(emptied, start + tile_done)
                        products(r, *arg)
                    elif stage == "spread":
                        h, m = arg
                        spread_ids(m, bass.ds((2 * r + 1 + h) * HALF, HALF))
                    elif stage == "lookup":
                        h, m = arg
                        lookup(start, (h * NL + m) % 2, m, (2 * r + 2 + h) * NL + m + 1,
                               bass.ds((2 * r + 1 + h) * HALF, HALF))
                    elif stage == "unblock":
                        h, b = arg
                        unblock(2 * r + 1 + h, start, b)
                        after = start + use[0]
                    elif stage == "pairs":
                        transpose_pairs(start, after, arg[1])
                    elif stage == "layer1":
                        h, n = arg
                        layer1(2 * r + 1 + h, start, n)
                    elif stage == "layer2":
                        h, n = arg
                        layer2(2 * r + 1 + h, start, n)
                        after = start + use[0]
                    elif stage == "layer3":
                        layer3(start, after)

            def transpose_ids(t, n):
                ps = claim(0)
                for i in range(n):
                    last = pe.transpose(ps[0:NTAB, i * P:(i + 1) * P], ids_f[:, t + i, :], ident[:])
                last.then_inc(filled_ids, 1)

            pe.wait_ge(const_ready, 3)
            for _ in range(WARM_UP):
                pe.transpose(gram[:, 0, 0, 0:P], ident[:], ident[:])
            pe.wait_ge(ids_f_ready, 1)
            transpose_ids(0, 2)
            transpose_ids(2, 4)
            pe.wait_ge(emptied, 1)
            pe.wait_ge(ident_r_ready, 1)
            col = slice(B - 2 * HALF, B - HALF)
            spread_ids(0, col)
            for t in range(6, NTILE - 2, 4):
                transpose_ids(t, 4)
            for m in range(NL):
                if m < NRAW:
                    lookup_raw(m, col)
                else:
                    pe.wait_ge(hi_ready, m - NRAW + 1)
                    pe.wait_ge(lo_ready, m - NRAW + 1)
                    lookup(0, m % 2, m, m + 1, col)
                for g in EARLY_ROWS_OF[m]:
                    transpose_rows(-1, 0, 2, g)
            transpose_ids(NTILE - 2, 2)
            pe.wait_ge(hi_ready, NL)
            pe.wait_ge(lo_ready, NL)
            pe.wait_ge(xt0_cleared, 1)
            play(-1, START, 0)
            pe.wait_ge(xt1_cleared, 1)
            use[0] = 0
            with pe.Fori(0, NROUND) as r:
                play(r, WHOLE, ring_start(r))
            use[0] = 0
            play(NROUND, LAST, ring_start(NROUND))
            play(NROUND, END, ring_start(NROUND))

        @block.scalar
        def _(act):
            use = [0]
            mlp_use = [0]

            def bank(start):
                n = use[0]
                use[0] += 1
                return ring[:, bank_of(start, n), :]

            def store_lookup(start, h, m, ready):
                act.wait_ge(looked_up, ready)
                act.copy(XT[h][:, :, LOOKUP_TABLES[m] + 1], bank(start)[:, 0:HALF]).then_inc(emptied, 1)

            def store_rows(r, start, t, g, early):
                h, q = divmod((t + 2) % 4, 2)
                xt = XT[h][:, q * TILE:(q + 1) * TILE, :]
                act.wait_ge(filled_rows, USES_X * (4 * r + t + 2) + g + 1)
                if g == 0 and t in (2, 4) and not early:
                    act.wait_ge(dense_lo, 2 * r + t // 2)
                ps = bank(start)
                for i, f0, step, n in runs([FEAT[row] for row in XGROUPS[g]]):
                    last = act.copy(xt[:, :, f0:f0 + step * (n - 1) + 1:step].rearrange("d s f -> d f s"),
                                    ps[:, i * P:(i + n) * P].rearrange("d (f s) -> d f s", f=n))
                last.then_inc(emptied, 1)

            def store_products(r, h, s):
                act.wait_ge(gram_ready, STEPS * (2 * r + 1 + h) + s + 1)
                act.copy(*product_views(s, 2))
                act.copy(*product_views(s, 3)).then_inc(gram_act, 1)

            def mlp_bank(start, mlp0):
                act.wait_ge(filled_mlp, mlp0 + mlp_use[0] + 1)
                mlp_use[0] += 1
                return bank(start)

            def store_unblocked(start, mlp0, b):
                ps = mlp_bank(start, mlp0)
                for i, u in enumerate(COUPLES_OF[b]):
                    for a, p0 in ((2 * u, 0), (2 * u + 1, NI)):
                        n = NA - a
                        blk = ps[p0:p0 + NI, i * P:(i + 1) * P].rearrange("p (j b) -> p j b", j=QUAD)
                        last = act.copy(pairs[:, :, PAIR0[a]:PAIR0[a] + n], blk[:, :, a + 1:F])
                last.then_inc(emptied, 1)

            def store_pairs(H, start, mlp0, k):
                if k == 0:
                    act.wait_ge(y_stored, 16 * H)
                k0, w = K_PAIR[k]
                ps = mlp_bank(start, mlp0)
                act.copy(x_split[0][0:w, 1 + k, :], ps[0:w, 0:HALF])
                act.copy(pairs_t[0:w, k, :], ps[0:w, 0:HALF]).then_inc(emptied, 1)

            def store_layer(start, mlp0, h_next, bias, n):
                act.wait_ge(weights_landed, 16 * N_WEIGHTS)
                ps = mlp_bank(start, mlp0)
                act.activation(h_next[:, n, :], ps[:, 0:HALF], ACT.Relu, bias=bias[:, n:n + 1]).then_inc(emptied, 1)

            def store_y(H, start, mlp0):
                ps = mlp_bank(start, mlp0)
                act.copy(y_row.rearrange("o (i j) -> o j i", j=QUAD),
                         ps[0:1, 0:HALF].rearrange("o (j i) -> o j i", j=QUAD)).then_inc(emptied, 1)
                act.wait_ge(emptied, start + use[0])
                act.dma_start(out[bass.ds((H - 1) * HALF, HALF), :].rearrange("s o -> o s"), y_row).then_inc(y_stored, 16)

            def play(r, kind, start, mlp0):
                for stage, *arg in stages(kind):
                    if stage == "rows":
                        store_rows(r, start, *arg, kind == START)
                    elif stage == "products":
                        store_products(r, *arg)
                    elif stage == "lookup":
                        h, m = arg
                        store_lookup(start, h, m, (2 * r + 2 + h) * NL + m + 1)
                    elif stage == "unblock":
                        store_unblocked(start, mlp0, arg[1])
                    elif stage == "pairs":
                        h, k = arg
                        store_pairs(2 * r + 1 + h, start, mlp0, k)
                    elif stage == "layer1":
                        store_layer(start, mlp0, h1, b1, arg[1])
                    elif stage == "layer2":
                        store_layer(start, mlp0, h2, b2, arg[1])
                    elif stage == "layer3":
                        store_y(2 * r + 1 + arg[0], start, mlp0)

            def store_ids(col, n, ready):
                act.wait_ge(filled_ids, ready)
                act.copy(ids_t[:, col:col + n], bank(0)[0:NTAB, 0:n]).then_inc(emptied, 1)

            store_ids(B - 2 * HALF, HALF, 1)
            for t in range(2, NTILE - 2, 4):
                store_ids((t - 2) * P, 4 * P, (t + 2) // 4 + 1)
            n_split = 0
            weights = weight_parts(w1[0], w2[0])
            for m in range(NL):
                for j in SPLIT_ORDER[n_split:(m + 1) * (NL // 2 + 1)]:
                    act.wait_ge(raw_landed[j], 16)
                    act.copy(table_hi[:, j], raw[:, j]).then_inc(hi_ready, 1)
                    n_split += 1
                store_lookup(0, 0, m, m + 1)
                for g in EARLY_ROWS_OF[m]:
                    store_rows(-1, 0, 2, g, True)
                if m == NL - 3:
                    act.wait_ge(weights_landed, 16 * N_WEIGHTS)
                    for part, raw_part in weights[0:2]:
                        act.copy(part, raw_part).then_inc(weights_hi, 1)
            store_ids(B - 2 * HALF, HALF, NTILE // 4 + 1)
            act.wait_ge(w1_ready, 1)
            for part, raw_part in weights[2:4]:
                act.copy(part, raw_part).then_inc(weights_hi, 1)
            act.wait_ge(places_free, 1)
            play(-1, START, 0, 0)
            act.wait_ge(weights_lo, WEIGHT_PARTS)
            act.sem_inc(y_stored, 16)
            use[0] = mlp_use[0] = 0
            with act.Fori(0, NROUND) as r:
                play(r, WHOLE, ring_start(r), mlp_start(r))
            use[0] = mlp_use[0] = 0
            play(NROUND, LAST, ring_start(NROUND), mlp_start(NROUND))
            play(NROUND, END, ring_start(NROUND), mlp_start(NROUND))
            act.wait_ge(y_stored, 16 * (2 * NROUND + 3))

        @block.vector
        def _(dve):
            def one_hot(buf, ready, free):
                dve.wait_ge(idb_ready, ready)
                if free is not None:
                    dve.wait_ge(looked_up, free)
                dve.tensor_tensor(onehot[:, buf], idb[0:VP, 0:HALF].unsqueeze(1).to_broadcast([VP, KT, HALF]),
                                  vrow[:].unsqueeze(2).to_broadcast([VP, KT, HALF]), ALU.is_equal).then_inc(onehot_ready, 1)

            def lower_part(n):
                m = SPLIT_ORDER[n]
                dve.wait_ge(hi_ready, n + 1)
                dve.tensor_tensor(table_lo[:, m], raw[:, m], table_hi[:, m].bitcast(F32), ALU.subtract).then_inc(lo_ready, 1)

            dve.wait_ge(ids_landed, 16)
            dve.tensor_copy(ids_f[:], ids_all[:]).then_inc(ids_f_ready, 1)
            dve.wait_ge(const_ready, 3)
            dve.tensor_copy(ident_r[:], ident[:]).then_inc(ident_r_ready, 1)
            dve.tensor_copy(vrow[:], vrow_i[:]).then_inc(vrow_ready, 1)
            dve.memset(XT[0][:, :, F:QW], 0.0).then_inc(xt0_cleared, 1)
            dve.wait_ge(vrow_ready, 1)
            for m in range(NL):
                if m >= 2:
                    lower_part(m - 2)
                one_hot(m % 2, m + 1, m - 1 if m >= 2 else None)
            dve.wait_ge(weights_landed, 16 * N_WEIGHTS)
            dve.tensor_tensor(w1_dense_raw, w1_dense_raw, w1_again, ALU.add).then_inc(w1_ready, 1)
            for n in range(NL - 2, NL):
                lower_part(n)

            weights = list(zip(weight_parts(w1[1], w2[1]), weight_parts(w1[0], w2[0])))

            def lower_weights(i):
                (part, raw_part), (hi, _) = weights[i]
                dve.wait_ge(weights_hi, i + 1)
                dve.tensor_tensor(part, raw_part, hi.bitcast(F32), ALU.subtract).then_inc(weights_lo, 1)

            for i in range(3):
                lower_weights(i)
            dve.wait_ge(looked_up, NRAW)
            dve.wait_ge(lo_ready, NL)
            dve.wait_ge(weights_lo, 3)
            dve.wait_ge(filled_ids, NTILE // 4 + 1)
            dve.sem_inc(places_free, 1)

            def split_dense(H, h, start, uses):
                dve.wait_ge(emptied, start + uses)
                x = XT[h][:, :, 0].rearrange("d (i j) -> d j i", j=QUAD)
                hi, lo = (part[:, 0, :].rearrange("d (j i) -> d j i", j=QUAD) for part in x_split)
                dve.tensor_copy(hi, x).then_inc(dense_hi, 1)
                dve.wait_ge(dense_hi, H)
                dve.tensor_tensor(lo, x, hi.bitcast(F32), ALU.subtract).then_inc(dense_lo, 1)

            def split_pairs(start, uses, k):
                dve.wait_ge(emptied, start + uses)
                w = K_PAIR[k][1]
                dve.tensor_tensor(x_split[1][0:w, 1 + k], pairs_t[0:w, k], x_split[0][0:w, 1 + k].bitcast(F32),
                                  ALU.subtract).then_inc(pairs_lo, 1)

            def split_h1(H, start, uses):
                dve.wait_ge(emptied, start + uses)
                for k in range(H1 // P + 1):
                    if k < H1 // P:
                        dve.tensor_copy(h1_split[0][:, k], h1[:, k]).then_inc(h1_hi, 1)
                    if k > 0:
                        dve.wait_ge(h1_hi, (H - 1) * (H1 // P) + k)
                        dve.tensor_tensor(h1_split[1][:, k - 1], h1[:, k - 1], h1_split[0][:, k - 1].bitcast(F32),
                                          ALU.subtract).then_inc(h1_lo, 1)

            def play(r, kind, start):
                uses = 0
                for stage, *arg in stages(kind):
                    uses += stage in RING_STAGES
                    if stage == "products":
                        h, s = arg
                        dve.wait_ge(gram_ready, STEPS * (2 * r + 1 + h) + s + 1)
                        dve.tensor_copy(*product_views(s, 0))
                        dve.tensor_copy(*product_views(s, 1)).then_inc(gram_dve, 1)
                    elif stage == "spread" or stage == "lookup" and arg[1] + 1 < NL:
                        h, m = arg
                        if stage == "lookup":
                            m += 1
                        n = (2 * r + 2 + h) * NL + m
                        one_hot((h * NL + m) % 2, n + 1, n - 1)
                    elif stage == "leftovers":
                        lower_weights(3)
                        dve.memset(XT[1][:, :, F:QW], 0.0).then_inc(xt1_cleared, 1)
                    elif stage == "dense":
                        split_dense(2 * r + 1 + arg[0], arg[0], start, uses)
                    elif stage == "pairs":
                        split_pairs(start, uses, arg[1])
                    elif stage == "layer1" and arg[1] == H1 // P - 1:
                        split_h1(2 * r + 1 + arg[0], start, uses)
                return uses

            play(-1, START, 0)
            with dve.Fori(0, NROUND) as r:
                play(r, WHOLE, ring_start(r))
            uses = play(NROUND, LAST, ring_start(NROUND))
            play(NROUND, END, ring_start(NROUND) + uses)


N_WEIGHTS = 9
WEIGHT_PARTS = 4


_OUTS = [((2048, 1), 'float32')]
_INS = (["r_dense_features", "ids"] + [f"tbl_{i}" for i in range(26)]
        + ["W_top1", "b_top1", "W_top2", "b_top2", "W_top3"])


def kernel(**inputs):
    import numpy as np
    import concourse.bacc as bacc
    from concourse import mybir as mb
    from concourse.bass_utils import run_bass_kernel_spmd

    nc = bacc.Bacc("TRN2", target_bir_lowering=False, num_devices=1)
    arrays, aps = {}, {}
    for name in _INS:
        a = np.ascontiguousarray(inputs[name])
        arrays[f"in_{name}"] = a
        aps[name] = nc.dram_tensor(f"in_{name}", a.shape, mb.dt.from_np(a.dtype), kind="ExternalInput").ap()
    shape, dtype = _OUTS[0]
    out = nc.dram_tensor("out_y", shape, mb.dt.from_np(np.dtype(dtype)), kind="ExternalOutput").ap()
    build(nc, aps, out)
    r = run_bass_kernel_spmd(nc, [arrays], core_ids=[0])
    return r.results[0]["out_y"]
```
